# Optimizing a Trainium2 kernel written in Bass

```python
import numpy as np
import jax
import jax.numpy as jnp

def _softmax(x, axis=-1):
    return jax.nn.softmax(x, axis=axis)

def _gelu(x):
    return jax.nn.gelu(x, approximate=True)

def _silu(x):
    return jax.nn.silu(x)

def _sigmoid(x):
    return jax.nn.sigmoid(x)

def _layernorm(x, axis=-1, eps=1e-05):
    m = jnp.mean(x, axis=axis, keepdims=True)
    v = jnp.var(x, axis=axis, keepdims=True)
    return (x - m) / jnp.sqrt(v + eps)

def _scatter_add(tgt, idx, src, axis=0):
    return tgt.at[idx].add(src)

def _segment_sum(src, seg, n):
    return jax.ops.segment_sum(src, seg, n)
kernel_name = 'mk_xattn_ffn_d1_seqx_r4_635667'

def setup_inputs(seed: int=0):
    np.random.seed(seed)
    _w = jnp.asarray

    def _rec_inputs():
        import jax
        import jax.numpy as jnp
        _rk = jax.random.key(seed)
        x = -0.0003929 + 0.9999 * jax.random.normal(jax.random.fold_in(_rk, 1), (2, 1024, 256), jnp.float32)
        _lenS = 1024 - jax.random.randint(jax.random.fold_in(_rk, 7), (2,), 0, max(1, 1024 // 4) + 1, jnp.int32)
        _lenS2 = 64 - jax.random.randint(jax.random.fold_in(_rk, 8), (2,), 0, max(1, 64 // 4) + 1, jnp.int32)
        _ctx_1024P = jax.random.normal(jax.random.fold_in(_rk, 11), (2, 16, 256), jnp.float32)
        _ctx_1024c = jax.random.dirichlet(jax.random.fold_in(_rk, 511), 0.3 * jnp.ones((16,), jnp.float32), (2, 64))
        _ctx_1024t = jnp.einsum('bsk,bkd->bsd', _ctx_1024c, _ctx_1024P)
        _ctx_1024t = _ctx_1024t * jax.lax.rsqrt(jnp.mean(jnp.square(_ctx_1024t)) + 1e-12) * 0.953939
        ctx_1024 = 2.81802e-05 + 1.00001 * (_ctx_1024t + 0.3 * jax.random.normal(jax.random.fold_in(_rk, 611), (2, 64, 256), jnp.float32))
        return (x, ctx_1024)
    x, ctx_1024 = _rec_inputs()

    def _L0_xattn_setup():
        import jax, jax.numpy as jnp
        import numpy as np
        B, S, C = (8, 512, 256)
        key = jax.random.key(seed)
        ks = jax.random.split(key, 9)
        scale = 1.0 / np.sqrt(C)
        return {'x1': jax.random.normal(ks[0], (B, S, C), jnp.float32), 'x2': jax.random.normal(ks[1], (B, S, C), jnp.float32), 'x3': jax.random.normal(ks[2], (B, S, C), jnp.float32), 'Wq': jax.random.normal(ks[3], (C, C), jnp.float32) * scale, 'bq': jax.random.normal(ks[4], (C,), jnp.float32) * scale, 'Wk': jax.random.normal(ks[5], (C, C), jnp.float32) * scale, 'bk': jax.random.normal(ks[6], (C,), jnp.float32) * scale, 'Wv': jax.random.normal(ks[7], (C, C), jnp.float32) * scale, 'bv': jax.random.normal(ks[8], (C,), jnp.float32) * scale}
    _L0_xattn_all = _L0_xattn_setup()
    _L0_xattn_in = {k: v for k, v in _L0_xattn_all.items() if k in ('Wq', 'bq', 'Wk', 'bk', 'Wv', 'bv')}
    del _L0_xattn_all

    def _L0_ffn_setup():
        import jax, jax.numpy as jnp
        import numpy as np
        B, T, DIM, H, DH, TOPK = (4, 512, 256, 8, 64, 3)
        key = jax.random.key(seed)
        ks = jax.random.split(key, 6)
        x = jax.random.normal(ks[0], (B, T, DIM), dtype=jnp.float32)
        sc = 1.0 / np.sqrt(DIM)
        Wq = jax.random.normal(ks[1], (DIM, H * DH), dtype=jnp.float32) * sc
        Wkv = jax.random.normal(ks[2], (DIM, 2 * H * DH), dtype=jnp.float32) * sc
        Ws = jax.random.normal(ks[3], (DIM, H), dtype=jnp.float32) * sc
        Wo = jax.random.normal(ks[4], (H, DH, DIM), dtype=jnp.float32) * (1.0 / np.sqrt(DH))
        bo = jax.random.normal(ks[5], (H, DIM), dtype=jnp.float32) * 0.01
        return {'x': x, 'Wq': Wq, 'Wkv': Wkv, 'Ws': Ws, 'Wo': Wo, 'bo': bo}
    _L0_ffn_all = _L0_ffn_setup()
    _L0_ffn_in = {k: v for k, v in _L0_ffn_all.items() if k in ('Wq', 'Wkv', 'Ws', 'Wo', 'bo')}
    del _L0_ffn_all
    return {'x': x, 'ctx_1024': ctx_1024, 'L0_xattn_Wq': _L0_xattn_in['Wq'], 'L0_xattn_bq': _L0_xattn_in['bq'], 'L0_xattn_Wk': _L0_xattn_in['Wk'], 'L0_xattn_bk': _L0_xattn_in['bk'], 'L0_xattn_Wv': _L0_xattn_in['Wv'], 'L0_xattn_bv': _L0_xattn_in['bv'], 'L0_ffn_Wq': _L0_ffn_in['Wq'], 'L0_ffn_Wkv': _L0_ffn_in['Wkv'], 'L0_ffn_Ws': _L0_ffn_in['Ws'], 'L0_ffn_Wo': _L0_ffn_in['Wo'], 'L0_ffn_bo': _L0_ffn_in['bo']}

def reference(x, ctx_1024, L0_xattn_Wq, L0_xattn_bq, L0_xattn_Wk, L0_xattn_bk, L0_xattn_Wv, L0_xattn_bv, L0_ffn_Wq, L0_ffn_Wkv, L0_ffn_Ws, L0_ffn_Wo, L0_ffn_bo):
    import jax
    import jax.numpy as jnp

    def _L0_xattn_ref(x1, x2, x3, Wq, bq, Wk, bk, Wv, bv):
        import jax, jax.numpy as jnp
        import numpy as np
        B, S, C = (8, 512, 256)
        q = jnp.einsum('bsc,dc->bsd', x1, Wq) + bq
        k = jnp.einsum('bsc,dc->bsd', x2, Wk) + bk
        v = jnp.einsum('bsc,dc->bsd', x3, Wv) + bv
        scores = jnp.einsum('bqd,bkd->bqk', q, k)
        attn = jax.nn.softmax(scores, axis=-1)
        return jnp.einsum('bqk,bkd->bqd', attn, v)

    def _L0_ffn_ref(x, Wq, Wkv, Ws, Wo, bo):
        import jax, jax.numpy as jnp
        import numpy as np
        B, T, DIM, H, DH, TOPK = (4, 512, 256, 8, 64, 3)
        b, t, _ = x.shape
        s = jax.nn.sigmoid(x @ Ws)
        vals, idx = jax.lax.top_k(s, TOPK)
        bi = jnp.arange(b)[:, None, None]
        ti = jnp.arange(t)[None, :, None]
        scores = jnp.zeros_like(s).at[bi, ti, idx].set(vals)
        q = (x @ Wq).reshape(b, t, H, DH).transpose(0, 2, 1, 3)
        kv = (x @ Wkv).reshape(b, t, 2, H, DH).transpose(2, 0, 3, 1, 4)
        k, v = (kv[0], kv[1])
        scale = DH ** (-0.5)
        attn = jax.nn.softmax(jnp.einsum('bhid,bhjd->bhij', q * scale, k), axis=-1)
        out = jnp.einsum('bhij,bhjd->bhid', attn, v)
        proj = jnp.einsum('bhtd,hde->bhte', out, Wo) + bo[None, :, None, :]
        return jnp.einsum('bhte,bth->bte', proj, scores)
    x = x + _L0_xattn_ref(_layernorm(x, axis=-1), ctx_1024, ctx_1024, L0_xattn_Wq, L0_xattn_bq, L0_xattn_Wk, L0_xattn_bk, L0_xattn_Wv, L0_xattn_bv)
    x = x + _L0_ffn_ref(_layernorm(x, axis=-1), L0_ffn_Wq, L0_ffn_Wkv, L0_ffn_Ws, L0_ffn_Wo, L0_ffn_bo)
    return x

_drawn_inputs = setup_inputs


def setup_inputs(seed=0):
    import zlib

    import numpy as np

    out = dict(_drawn_inputs(seed))
    spreads = {}
    factors = {'L0_xattn_bk': 8.0, 'L0_ffn_bo': 7.197}
    for name, (base, spread) in spreads.items():
        noise = np.random.default_rng([zlib.crc32(name.encode()), seed]).standard_normal(out[name].shape)
        drawn = base * np.exp(spread * noise) if base else spread * noise
        out[name] = jnp.asarray(drawn.astype(out[name].dtype))
    for name, factor in factors.items():
        out[name] = (out[name] * factor).astype(out[name].dtype)
    return out
```

```python
from contextlib import ExitStack

import concourse.bass as bass
from concourse import mybir

P = 128
F32 = mybir.dt.float32
F32R = mybir.dt.float32r
ALU = mybir.AluOpType
ACT = mybir.ActivationFunctionType
AX = mybir.AxisListType

LN_EPS = 1e-5
TOP_K = 3


def build(nc, x, ctx_in, wq1, bq1, wk1, bk1, wv1, bv1, wq2, wkv2, ws2, wo2, bo2, out):
    B, T, C = x.shape
    KEYS = ctx_in.shape[1]
    H, DH, _ = wo2.shape
    HD = H * DH
    CC = C // P
    NT = T // P
    G = B * NT
    U = B * H
    SCALE = float(DH) ** -0.5
    HALF = 512
    NH = T // HALF
    ONES = DH
    VLO = DH + 2
    VW = 2 * DH + 2
    NPH = 4
    LAG = 2
    MAX_SLOTS = (2, 3, 4, 5)
    assert B == 2 and C == CC * P and B * KEYS == P and 2 * DH == P and U * NT == P and NT == 8

    base_d = nc.dram_tensor("base_d", (P, G, C), F32, kind="Internal").ap()
    v_d = nc.dram_tensor("v_d", (B, H, P, NT * DH), F32, kind="Internal").ap()
    gate_d = nc.dram_tensor("gate_d", (P, P), F32, kind="Internal").ap()
    weight_d = nc.dram_tensor("weight_d", (B, T), F32, kind="Internal").ap()

    with ExitStack() as top:
        sem_names = {}

        def sem(name):
            sem_names[name] = top.enter_context(nc.semaphore(name))
            return sem_names[name]

        def sb(name, shape, dt=F32, stack=top):
            return stack.enter_context(nc.sbuf_tensor(name, shape, dt))

        ident = sb("ident", [P, P])
        ones_row = sb("ones_row", [1, P])
        zero = sb("zero", [P, 1])
        stats = sb("stats", [P, G, 6])
        mean_var = sb("mean_var", [P, G, 2])
        rstd = sb("rstd", [P, G])
        wqk_raw = sb("wqk_raw", [P, CC, P])
        wqk_hi = sb("wqk_hi", [P, CC, P], F32R)
        wqk_lo = sb("wqk_lo", [P, CC, P], F32R)
        ws_raw = sb("ws_raw", [P, CC, H])
        ws_hi = sb("ws_hi", [P, CC, H], F32R)
        ws_lo = sb("ws_lo", [P, CC, H], F32R)
        qk_hi = sb("qk_hi", [P, T], F32R)
        qk_lo = sb("qk_lo", [P, T], F32R)
        kk = [sb(f"kk{b}", [P, T], F32R) for b in range(B)]
        qq = [sb(f"qq{b}", [P, T], F32R) for b in range(B)]
        k1 = [sb(f"k1{b}", [P, T], F32R) for b in range(B)]
        qm = [sb(f"qm{b}", [P, T], F32R) for b in range(B)]
        v_raw = sb("v_raw", [P, NT, DH])
        v_st = [sb(f"v_st{b}", [P, NT, VW], F32R) for b in range(B)]
        row_max = sb("row_max", [P, B, NT])
        neg_max = sb("neg_max", [NT, 2, P], F32R)
        den = sb("den", [NT, P])
        rden = sb("rden", [NT, P])
        gate = sb("gate", [NT, P])
        weight = sb("weight", [NT, P])
        mx1 = sb("mx1", [P, G])
        sum1 = sb("sum1", [P, G])
        rsum1 = sb("rsum1", [P, G])
        g_exp = sb("g_exp", [P, G, H])
        g_sig = sb("g_sig", [P, G, H])
        g_rank = sb("g_rank", [P, G, H])
        g_keep = sb("g_keep", [P, G, H])
        g_unit = sb("g_unit", [P, P])
        g_unitT = sb("g_unitT", [P, P])
        before = sb("before", [P, H, H])

        def overlay(*stages):
            widest, got = 0, []
            for named in stages:
                size = sum(w * 4 for _, w in ((n, _width(s)) for n, s, _ in named))
                widest = max(widest, size)
                with ExitStack() as own:
                    got.append([sb(n, s, d, own) for n, s, d in named])
            sb(f"room{len(rooms)}", [P, widest // 4])
            rooms.append(widest)
            return got

        def _width(shape):
            n = 1
            for s in shape[1:]:
                n *= s
            return n

        rooms = []
        (xT_hi, xT_lo), (wo_raw, wo_hi, wo_lo) = overlay(
            [("xT_hi", [P, CC, B * T], F32R), ("xT_lo", [P, CC, B * T], F32R)],
            [("wo_raw", [P, H, C], F32), ("wo_hi", [P, H, C], F32R), ("wo_lo", [P, H, C], F32R)])
        (x_sb, xn, xnT, sT_raw, sT), (o_st,) = overlay(
            [("x_sb", [P, G, C], F32), ("xn", [P, G, C], F32), ("xnT", [P, CC, B * T], F32),
             ("sT_raw", [H, B * T], F32), ("sT", [H, B * T], F32)],
            [("o_st", [P, B, H, T], F32R)])
        (ctx_sb, ctxT, wk_sb, wv_sb, wq_sb, wkT, wvT, kT1, foldT, fold_b, v1, sub1, prob1, probT,
         bk_sb, bq_sb, bq_col, bv_sb, bo_sb, wv_raw, wv_hi, wv_lo, v_stage), \
            (prob, prob_hi, prob_lo, num, wide, o_hi, o_lo), (base,) = overlay(
            [("ctx_sb", [P, C], F32), ("ctxT", [P, CC, P], F32), ("wk_sb", [P, CC, C], F32),
             ("wv_sb", [P, CC, C], F32), ("wq_sb", [P, CC, C], F32), ("wkT", [P, CC, C], F32),
             ("wvT", [P, CC, C], F32), ("kT1", [P, CC, P], F32), ("foldT", [P, CC, P], F32),
             ("fold_b", [1, P], F32), ("v1", [P, C], F32), ("sub1", [P, G, KEYS], F32),
             ("prob1", [P, NT, P], F32), ("probT", [P, NT, P], F32), ("bk_sb", [1, C], F32),
             ("bq_sb", [1, C], F32), ("bq_col", [P, CC], F32), ("bv_sb", [1, C], F32), ("bo_sb", [H, C], F32),
             ("wv_raw", [P, CC, HD], F32), ("wv_hi", [P, CC, HD], F32R),
             ("wv_lo", [P, CC, HD], F32R), ("v_stage", [P, 2, HD], F32)],
            [("prob", [P, 2, T], F32), ("prob_hi", [P, NPH, T], F32R),
             ("prob_lo", [P, 2, T], F32R), ("num", [DH + 1, T], F32), ("wide", [DH, T], F32),
             ("o_hi", [DH, T], F32R), ("o_lo", [DH, T], F32R)],
            [("base", [P, G, C], F32)])

        psS = top.enter_context(nc.psum_tensor("psS", [P, 2, T], F32))
        psM = top.enter_context(nc.psum_tensor("psM", [P, T], F32))
        psO = top.enter_context(nc.psum_tensor("psO", [P, T], F32))

        def bank(n):
            return psS[:, n // 2, (n % 2) * HALF:(n % 2 + 1) * HALF]

        x_in = [sem(f"x_in{i}") for i in range(4)]
        ctx_landed = sem("ctx_landed")
        wqk_landed = sem("wqk_landed")
        wv_landed = sem("wv_landed")
        small_landed = sem("small_landed")
        consts_set = sem("consts_set")
        consts_done = sem("consts_done")
        stats_done = sem("stats_done")
        var_done = sem("var_done")
        eps_added = sem("eps_added")
        std_done = sem("std_done")
        rstd_done = sem("rstd_done")
        xn_done = sem("xn_done")
        ctx_turned = sem("ctx_turned")
        ctx_kept = sem("ctx_kept")
        kv1_done = sem("kv1_done")
        kv1_kept = sem("kv1_kept")
        fold_done = sem("fold_done")
        fold_kept = sem("fold_kept")
        xn_turned = sem("xn_turned")
        xnT_kept = sem("xnT_kept")
        xT_hi_kept = sem("xT_hi_kept")
        xT_lo_kept = sem("xT_lo_kept")
        sc1_done = sem("sc1_done")
        max1_done = sem("max1_done")
        sub1_done = sem("sub1_done")
        exp1_done = sem("exp1_done")
        sum1_done = sem("sum1_done")
        rsum1_done = sem("rsum1_done")
        prob1_turned = sem("prob1_turned")
        probT_kept = sem("probT_kept")
        out1_done = sem("out1_done")
        x1_done = sem("x1_done")
        wv_split = sem("wv_split")
        v_done = sem("v_done")
        v_kept = sem("v_kept")
        v_stored = [sem(f"v_stored{i}") for i in range(2)]
        ws_split = sem("ws_split")
        logits_done = sem("logits_done")
        logits_kept = sem("logits_kept")
        logits_turned = sem("logits_turned")
        gate_exp = sem("gate_exp")
        gate_step = sem("gate_step")
        gate_turned = sem("gate_turned")
        gate_kept = sem("gate_kept")
        gate_stored = sem("gate_stored")
        bias_done = sem("bias_done")
        base_done = sem("base_done")
        base_stored = sem("base_stored")

        wqk_split = sem("wqk_split")
        qk_done = sem("qk_done")
        qk_hi_kept = sem("qk_hi_kept")
        qk_lo_kept = sem("qk_lo_kept")
        stacks_free = sem("stacks_free")
        pairs_set = sem("pairs_set")
        rest_set = sem("rest_set")
        v_fetched = sem("v_fetched")
        v_split = sem("v_split")
        max_scores = sem("max_scores")
        max_found = sem("max_found")
        max_turned = sem("max_turned")
        max_split = sem("max_split")
        max_set = sem("max_set")
        scores_done = sem("scores_done")
        exp_done = sem("exp_done")
        hi_done = sem("hi_done")
        lo_done = sem("lo_done")
        pv_done = sem("pv_done")
        num_kept = sem("num_kept")
        den_moved = sem("den_moved")
        gate_fetched = sem("gate_fetched")
        rden_done = sem("rden_done")
        weight_done = sem("weight_done")
        weight_stored = sem("weight_stored")
        wide_fetched = sem("wide_fetched")
        out_split = sem("out_split")
        o_set = sem("o_set")
        wo_landed = sem("wo_landed")
        wo_split = sem("wo_split")
        base_fetched = sem("base_fetched")
        proj_done = sem("proj_done")
        final_done = sem("final_done")
        out_stored = sem("out_stored")

        x_tiles = x.rearrange("b (t p) c -> p (b t) c", p=P)
        out_tiles = out.rearrange("b (t p) c -> p (b t) c", p=P)
        wq_heads = wq2.rearrange("(cc p) n -> p cc n", p=P)
        wkv_heads = wkv2.rearrange("(cc p) n -> p cc n", p=P)

        def unit(h, b):
            return B * h + b

        block = top.enter_context(nc.Block())

        @block.sync
        def _(sp):
            for i in range(4):
                w = G // 4
                sp.dma_start(x_sb[:, i * w:(i + 1) * w, :], x_tiles[:, i * w:(i + 1) * w, :]).then_inc(x_in[i], 16)
                if i == 0:
                    sp.dma_start(ctx_sb[:, :], ctx_in.rearrange("b k c -> (b k) c")).then_inc(ctx_landed, 16)
                    for w_sb, w_in in ((wk_sb, wk1), (wv_sb, wv1), (wq_sb, wq1)):
                        sp.dma_start(w_sb[:, :, :], w_in.rearrange("(dd p) c -> p dd c", p=P)).then_inc(ctx_landed, 16)
                    for b_sb, b_in in ((bk_sb, bk1), (bq_sb, bq1), (bv_sb, bv1)):
                        sp.dma_start(b_sb[:, :], b_in.rearrange("(a c) -> a c", a=1)).then_inc(ctx_landed, 16)
            sp.dma_start(ws_raw[:, :, :], ws2.rearrange("(cc p) h -> p cc h", p=P)).then_inc(small_landed, 16)
            sp.dma_start(bo_sb[:, :], bo2).then_inc(small_landed, 16)
            sp.dma_start(wv_raw[:, :, :], wkv_heads[:, :, HD:2 * HD]).then_inc(wv_landed, 16)

            def fetch_wqk(h):
                if not (isinstance(h, int) and h == 0):
                    sp.wait_ge(wqk_split, 2 * h)
                sp.dma_start(wqk_raw[:, :, 0:DH], wq_heads[:, :, bass.ds(h * DH, DH)]).then_inc(wqk_landed, 16)
                sp.dma_start(wqk_raw[:, :, DH:2 * DH], wkv_heads[:, :, bass.ds(h * DH, DH)]).then_inc(wqk_landed, 16)

            def stack_qk(v, b):
                sp.wait_ge(stacks_free, v + 1)
                sp.wait_ge(qk_lo_kept, v + 1)
                for dst, src in ((kk[b][0:DH, :], qk_hi[DH:P, :]), (kk[b][DH:P, :], qk_hi[DH:P, :]),
                                 (qq[b][0:DH, :], qk_hi[0:DH, :]), (qq[b][DH:P, :], qk_lo[0:DH, :])):
                    sp.dma_start(dst.bitcast(F32), src.bitcast(F32)).then_inc(pairs_set, 16)
                for dst, src in ((k1[b][0:DH, :], qk_lo[DH:P, :]), (qm[b][0:DH, :], qk_hi[0:DH, :])):
                    sp.dma_start(dst.bitcast(F32), src.bitcast(F32)).then_inc(rest_set, 16)

            def fetch_v(v, h, b):
                if not (isinstance(v, int) and v == 0):
                    sp.wait_ge(v_split, 2 * v)
                sp.dma_start(v_raw[:, :, :], v_d[b, bass.ds(h, 1)].rearrange("a p (t d) -> p (a t) d", d=DH)).then_inc(v_fetched, 16)

            def set_max(v, b):
                sp.wait_ge(max_split, 2 * (v + 1))
                for part in range(2):
                    sp.dma_start(qm[b][DH + part:DH + part + 1, :].bitcast(F32).rearrange("a (t p) -> a t p", p=P),
                                 neg_max[:, part, :].bitcast(F32)).then_inc(max_set, 16)

            def weigh(w, b):
                first = isinstance(w, int) and w == 0
                if not first:
                    sp.wait_ge(weight_done, w)
                sp.dma_start(gate[:, :], gate_d[bass.ds(w * NT, NT), :]).then_inc(gate_fetched, 16)
                sp.wait_ge(num_kept, w + 1)
                sp.dma_start(den[:, :], num[DH:DH + 1, :].rearrange("a (t p) -> a t p", p=P)).then_inc(den_moved, 16)
                sp.wait_ge(weight_done, w + 1)
                sp.dma_start(weight_d[b].rearrange("(t p) -> t p", p=P), weight[:, :]).then_inc(weight_stored, 16)
                sp.wait_ge(weight_stored, 16 * (w + 1))
                sp.dma_start(wide[:, :], weight_d[b:b + 1, :].broadcast_to([DH, T])).then_inc(wide_fetched, 16)

            def store_out(w, h, b):
                sp.wait_ge(out_split, 3 * (w + 1))
                for part, src in enumerate((o_hi, o_lo)):
                    sp.dma_start(o_st[part * DH:(part + 1) * DH, b, bass.ds(h, 1), :].bitcast(F32).rearrange("p a t -> p (a t)"),
                                 src[:, :].bitcast(F32)).then_inc(o_set, 16)

            fetch_wqk(0)
            for g in range(G):
                sp.wait_ge(v_kept, g + 1)
                sp.dma_start(v_d[g // NT].rearrange("h p (t d) -> p h t d", d=DH)[:, :, g % NT, :],
                             v_stage[:, g % 2, :].rearrange("p (h d) -> p h d", d=DH)).then_inc(v_stored[g % 2], 16)
                if g == 1:
                    stack_qk(0, 0)
            sp.wait_ge(gate_kept, 2)
            sp.dma_start(gate_d, g_unitT[:, :]).then_inc(gate_stored, 16)
            set_max(0, 0)
            for i in range(2):
                sp.wait_ge(v_stored[i], 16 * G // 2)
            fetch_v(0, 0, 0)
            sp.wait_ge(base_done, G)
            sp.dma_start(base_d, x_sb[:, :, :]).then_inc(base_stored, 16)
            sp.wait_ge(gate_stored, 16)
            sp.wait_ge(base_stored, 16)

            def head(h, first=False, last=False):
                for b in range(B):
                    u = unit(h, b)
                    if not (last and b == B - 1):
                        stack_qk(u + 1, (b + 1) % B)
                        fetch_v(u + 1, h + (b + 1) // B, (b + 1) % B)
                    if b == 0 and not last:
                        fetch_wqk(h + 1)
                    if not first:
                        store_out(u - 2, h - 1, b)
                    if not (first and b == 0):
                        weigh(u - 1, (b + 1) % B)
                    if not (last and b == B - 1):
                        set_max(u + 1, (b + 1) % B)

            head(0, first=True)
            with sp.Fori(1, H - 1) as h:
                head(h)
            head(H - 1, last=True)
            sp.wait_ge(qk_done, U)
            for part in range(2):
                sp.dma_start(wo_raw[part * DH:(part + 1) * DH, :, :], wo2.rearrange("h d c -> d h c")).then_inc(wo_landed, 16)
            weigh(U - 1, (U - 1) % B)
            sp.wait_ge(base_stored, 16)
            for b in range(B):
                store_out(U - B + b, H - 1, b)
            sp.wait_ge(o_set, 32 * U)
            sp.dma_start(base[:, :, :], base_d).then_inc(base_fetched, 16)
            for g in range(G):
                sp.wait_ge(final_done, g + 1)
                sp.dma_start(out_tiles[:, g, :], base[:, g, :]).then_inc(out_stored, 16)
            sp.wait_ge(out_stored, 16 * G)

        @block.gpsimd
        def _(pool):
            nc.gpsimd.memset(ident[:, :], 0.0).then_inc(consts_set, 1)
            nc.gpsimd.memset(ones_row[:, :], 1.0).then_inc(consts_done, 1)
            nc.gpsimd.memset(before[:, :, :], 1.0).then_inc(consts_set, 1)
            nc.gpsimd.memset(zero[:, :], 0.0).then_inc(consts_set, 1)
            pool.wait_ge(consts_set, 3)
            nc.gpsimd.affine_select(out=ident[:, :], in_=ident[:, :], compare_op=ALU.not_equal, fill=1.0,
                                    base=0, pattern=[[-1, P]], channel_multiplier=1).then_inc(consts_done, 1)
            nc.gpsimd.affine_select(out=before[:, :, :], in_=before[:, :, :], compare_op=ALU.is_gt, fill=0.0,
                                    base=0, pattern=[[1, H], [-1, H]], channel_multiplier=0).then_inc(consts_done, 1)
            for b in range(B):
                last = nc.gpsimd.memset(v_st[b][:, :, ONES:ONES + 2].bitcast(F32), 1.0)
            last.then_inc(consts_done, 1)

            def round_to(dst, src):
                return nc.gpsimd.tensor_tensor(dst, src, zero[:, :].unsqueeze(2).broadcast_to(src.shape), ALU.add)

            def split_wqk(h):
                pool.wait_ge(wqk_landed, 32 * (h + 1))
                if not (isinstance(h, int) and h == 0):
                    pool.wait_ge(qk_done, B * h)
                round_to(wqk_hi[:, :, :], wqk_raw[:, :, :]).then_inc(wqk_split, 1)
                pool.wait_ge(wqk_split, 2 * h + 1)
                nc.gpsimd.tensor_tensor(wqk_lo[:, :, :], wqk_raw[:, :, :], wqk_hi[:, :, :], ALU.subtract).then_inc(wqk_split, 1)

            def split_v(v, b):
                pool.wait_ge(v_fetched, 16 * (v + 1))
                if not (isinstance(v, int) and v < B):
                    pool.wait_ge(pv_done, NT * (v - 1))
                round_to(v_st[b][:, :, 0:DH], v_raw[:, :, :]).then_inc(v_split, 1)
                pool.wait_ge(v_split, 2 * v + 1)
                nc.gpsimd.tensor_tensor(v_st[b][:, :, VLO:VLO + DH], v_raw[:, :, :], v_st[b][:, :, 0:DH],
                                        ALU.subtract).then_inc(v_split, 1)

            def finish(w):
                pool.wait_ge(wide_fetched, 16 * (w + 1))
                if not (isinstance(w, int) and w == 0):
                    pool.wait_ge(o_set, 32 * w)
                nc.gpsimd.tensor_tensor(o_hi[:, :], num[0:DH, :], wide[:, :], ALU.mult).then_inc(out_split, 1)
                pool.wait_ge(out_split, 3 * w + 1)
                nc.gpsimd.tensor_tensor(num[0:DH, :], num[0:DH, :], wide[:, :], ALU.mult).then_inc(out_split, 1)
                pool.wait_ge(out_split, 3 * w + 2)
                nc.gpsimd.tensor_tensor(o_lo[:, :], num[0:DH, :], o_hi[:, :], ALU.subtract).then_inc(out_split, 1)

            split_wqk(0)
            pool.wait_ge(small_landed, 32)
            nc.gpsimd.tensor_copy(ws_hi[:, :, :], ws_raw[:, :, :]).then_inc(ws_split, 1)
            pool.wait_ge(ws_split, 1)
            nc.gpsimd.tensor_tensor(ws_lo[:, :, :], ws_raw[:, :, :], ws_hi[:, :, :], ALU.subtract).then_inc(ws_split, 1)
            split_v(0, 0)

            def head(h, first=False, last=False):
                for b in range(B):
                    u = unit(h, b)
                    if b == 0 and not last:
                        split_wqk(h + 1)
                    if not (last and b == B - 1):
                        split_v(u + 1, (b + 1) % B)
                    if not (first and b == 0):
                        finish(u - 1)

            head(0, first=True)
            with pool.Fori(1, H - 1) as h:
                head(h)
            head(H - 1, last=True)
            finish(U - 1)

        @block.scalar
        def _(act):
            act.wait_ge(ctx_turned, 1)
            act.copy(ctxT[:, :, :], psO[:, 0:C]).then_inc(ctx_kept, 1)
            act.copy(wkT[:, :, :], psO[:, HALF:HALF + CC * C]).then_inc(ctx_kept, 1)
            act.copy(wvT[:, :, :], psM[:, 0:CC * C]).then_inc(ctx_kept, 1)
            act.wait_ge(kv1_done, 1)
            for dd in range(CC):
                act.copy(kT1[:, dd, :], psO[:, dd * P:(dd + 1) * P]).then_inc(kv1_kept, 1)
            act.copy(bq_col[:, :], psM[:, HALF:HALF + CC]).then_inc(kv1_kept, 1)
            act.copy(v1[:, :], psO[:, HALF:HALF + C]).then_inc(kv1_kept, 1)
            act.wait_ge(fold_done, 1)
            act.copy(foldT[:, :, :], psM[:, 0:C]).then_inc(fold_kept, 1)
            act.copy(fold_b[:, :], psM[0:1, HALF:HALF + P]).then_inc(fold_kept, 1)

            def std(n):
                act.wait_ge(eps_added, n + 1)
                act.activation(rstd[:, :], rstd[:, :], ACT.Sqrt).then_inc(std_done, 1)

            std(0)
            for k in range(G // 2):
                act.wait_ge(xn_turned, k + 1)
                act.copy(xnT[:, :, 2 * k * P:(2 * k + 2) * P].rearrange("p c (g q) -> p g c q", q=P),
                         bank(k % 4).rearrange("p (g c q) -> p g c q", g=2, c=CC)).then_inc(xnT_kept, 1)
            act.wait_ge(sub1_done, 1)
            act.activation(prob1[:, :, :], sub1[:, :, :].rearrange("p g k -> p (g k)"), ACT.Exp).then_inc(exp1_done, 1)
            act.wait_ge(prob1_turned, 1)
            act.copy(probT[:, :, :], psS[:, 0, :]).then_inc(probT_kept, 1)
            std(1)
            for k in range(G // 2):
                act.wait_ge(xn_turned, G // 2 + k + 1)
                act.copy(xT_hi[:, :, 2 * k * P:(2 * k + 2) * P].rearrange("p c (g q) -> p g c q", q=P),
                         bank(k % 4).rearrange("p (g c q) -> p g c q", g=2, c=CC)).then_inc(xT_hi_kept, 1)

            def keep_qk_hi(z):
                act.wait_ge(qk_done, z + 1)
                if not (isinstance(z, int) and z == 0):
                    act.wait_ge(pairs_set, 64 * z)
                    act.wait_ge(rest_set, 32 * z)
                act.copy(qk_hi[:, :], psM[:, :]).then_inc(qk_hi_kept, 1)

            keep_qk_hi(0)
            for g in range(G):
                act.wait_ge(v_done, g + 1)
                if g >= 2:
                    act.wait_ge(v_stored[g % 2], 16 * (g // 2))
                act.copy(v_stage[:, g % 2, :], bank(g % 4)).then_inc(v_kept, 1)
                if g == 5:
                    keep_qk_hi(1)
            for c in range(4):
                act.wait_ge(logits_done, c + 1)
                act.copy(sT_raw[:, c * HALF:(c + 1) * HALF], bank(c)[0:H, :]).then_inc(logits_kept, 1)
            act.wait_ge(logits_turned, 1)
            act.activation(g_exp[:, :, :], psO[:, 0:G * H], ACT.Exp, scale=-1.0).then_inc(gate_exp, 1)
            act.wait_ge(gate_turned, 1)
            act.copy(sT[:, :], psS[0:H, :, :].rearrange("p a t -> p (a t)")).then_inc(gate_kept, 1)
            act.copy(g_unitT[:, :], psO[:, HALF:HALF + P]).then_inc(gate_kept, 1)

            def keep_num(w):
                act.wait_ge(pv_done, NT * (w + 1))
                if not (isinstance(w, int) and w == 0):
                    act.wait_ge(out_split, 3 * w)
                    act.wait_ge(den_moved, 16 * w)
                act.copy(num[:, :], psO[0:DH + 1, :]).then_inc(num_kept, 1)

            def head(h, first=False, last=False):
                for b in range(B):
                    u = unit(h, b)
                    for t in range(NT):
                        act.wait_ge(scores_done, NT * u + t + 1)
                        if not (first and b == 0 and t < 2):
                            act.wait_ge(lo_done, NT * u + t - 1)
                        act.activation(prob[:, t % 2, :], psS[:, t % 2, :], ACT.Exp, scale=SCALE).then_inc(exp_done, 1)
                        act.wait_ge(exp_done, NT * u + t + 1)
                        if not (first and b == 0 and t < NPH):
                            act.wait_ge(pv_done, NT * u + t - NPH + 1)
                        act.copy(prob_hi[:, t % NPH, :], prob[:, t % 2, :]).then_inc(hi_done, 1)
                        if t == 1 and not (first and b == 0):
                            keep_num(u - 1)
                        if t == 6 and not last:
                            keep_qk_hi(u + 2)

            head(0, first=True)
            with act.Fori(1, H - 1) as h:
                head(h)
            head(H - 1, last=True)
            keep_num(U - 1)
            act.wait_ge(wo_landed, 32)
            act.copy(wo_hi[:, :, :], wo_raw[:, :, :]).then_inc(wo_split, 1)

        @block.vector
        def _(dve):
            def norm_stats(n):
                for g in range(G):
                    if n == 0 and g % 4 == 0:
                        dve.wait_ge(x_in[g // 4], 16)
                    dve.bn_stats(stats[:, g, :], x_sb[:, g, :]).then_inc(stats_done, 1)
                    dve.wait_ge(stats_done, G * n + g + 1)
                    dve.bn_aggr(mean_var[:, g, :], stats[:, g, :]).then_inc(var_done, 1)
                dve.wait_ge(var_done, G * (n + 1))
                dve.tensor_scalar(rstd[:, :], mean_var[:, :, 1], LN_EPS, None, ALU.add).then_inc(eps_added, 1)
                dve.wait_ge(std_done, n + 1)
                dve.reciprocal(rstd[:, :], rstd[:, :]).then_inc(rstd_done, 1)
                dve.wait_ge(rstd_done, n + 1)

            def norm(g):
                dve.tensor_scalar(xn[:, g, :], x_sb[:, g, :], mean_var[:, g, 0:1], rstd[:, g:g + 1],
                                  ALU.subtract, ALU.mult).then_inc(xn_done, 1)

            for b in range(B):
                dve.memset(k1[b][DH:P, :].bitcast(F32), 1.0)
                dve.memset(qm[b][DH:P, :].bitcast(F32), 0.0).then_inc(stacks_free, 1)
            norm_stats(0)
            for g in range(G):
                norm(g)
            dve.wait_ge(sc1_done, 1)
            scores1 = psM[:, :].rearrange("p (g k) -> p g k", k=KEYS)
            dve.reduce_max(mx1[:, :], scores1, AX.X).then_inc(max1_done, 1)
            dve.wait_ge(max1_done, 1)
            dve.tensor_tensor(sub1[:, :, :], scores1, mx1[:, :].unsqueeze(2).broadcast_to([P, G, KEYS]),
                              ALU.subtract).then_inc(sub1_done, 1)
            dve.wait_ge(exp1_done, 1)
            dve.reduce_sum(sum1[:, :], prob1[:, :, :].rearrange("p t (b k) -> p (t b) k", k=KEYS), AX.X).then_inc(sum1_done, 1)
            dve.wait_ge(sum1_done, 1)
            dve.reciprocal(rsum1[:, :], sum1[:, :]).then_inc(rsum1_done, 1)
            dve.wait_ge(rsum1_done, 1)
            for j in range(G):
                t, b = divmod(j, B)
                g = b * NT + t
                dve.wait_ge(out1_done, j + 1)
                src = bank(2 + j % 4) if j % 4 < 2 else psO[:, (j % 4 - 2) * HALF:(j % 4 - 1) * HALF]
                dve.scalar_tensor_tensor(out=x_sb[:, g, :], in0=src[:, 0:C], scalar=rsum1[:, j:j + 1],
                                         in1=x_sb[:, g, :], op0=ALU.mult, op1=ALU.add).then_inc(x1_done, 1)
            dve.wait_ge(x1_done, G)
            norm_stats(1)

            def keep_xT_lo(k):
                dve.wait_ge(xT_hi_kept, k + 1)
                view = slice(2 * k * P, (2 * k + 2) * P)
                dve.tensor_tensor(xT_lo[:, :, view].rearrange("p c (g q) -> p g c q", q=P),
                                  bank(k % 4).rearrange("p (g c q) -> p g c q", g=2, c=CC),
                                  xT_hi[:, :, view].rearrange("p c (g q) -> p g c q", q=P),
                                  ALU.subtract).then_inc(xT_lo_kept, 1)

            for g in range(G):
                norm(g)
                if g >= 5 and g % 2:
                    keep_xT_lo((g - 5) // 2)
            for k in range((G - 4) // 2, G // 2):
                keep_xT_lo(k)
            dve.wait_ge(wv_landed, 16)
            dve.tensor_copy(wv_hi[:, :, :], wv_raw[:, :, :]).then_inc(wv_split, 1)
            dve.wait_ge(wv_split, 1)
            dve.tensor_tensor(wv_lo[:, :, :], wv_raw[:, :, :], wv_hi[:, :, :], ALU.subtract).then_inc(wv_split, 1)

            def keep_qk_lo(z):
                dve.wait_ge(qk_hi_kept, z + 1)
                dve.tensor_tensor(qk_lo[:, :], psM[:, :], qk_hi[:, :], ALU.subtract).then_inc(qk_lo_kept, 1)

            def find_max(v, b, t):
                dve.wait_ge(max_scores, NT * v + t + 1)
                dve.reduce_max(row_max[:, b, t:t + 1], psM[:, :], AX.X).then_inc(max_found, 1)

            def split_max(v):
                dve.wait_ge(max_turned, v + 1)
                if not (isinstance(v, int) and v == 0):
                    dve.wait_ge(max_set, 32 * v)
                dve.tensor_scalar(neg_max[:, 0, :], psM[0:NT, 0:P], -1.0, None, ALU.mult).then_inc(max_split, 1)
                dve.wait_ge(max_split, 2 * v + 1)
                dve.scalar_tensor_tensor(out=neg_max[:, 1, :], in0=psM[0:NT, 0:P], scalar=-1.0, in1=neg_max[:, 0, :],
                                         op0=ALU.mult, op1=ALU.subtract).then_inc(max_split, 1)

            keep_qk_lo(0)
            keep_qk_lo(1)
            dve.wait_ge(gate_exp, 1)
            dve.tensor_scalar(g_exp[:, :, :], g_exp[:, :, :], 1.0, None, ALU.add).then_inc(gate_step, 1)
            dve.wait_ge(gate_step, 1)
            dve.reciprocal(g_sig[:, :, :], g_exp[:, :, :]).then_inc(gate_step, 1)
            dve.wait_ge(gate_step, 2)
            ahead = xn[:, 0:4, :].rearrange("p g c -> p (g c)").rearrange("p (g h k) -> p g h k", h=H, k=H)
            tied = xn[:, 4:8, :].rearrange("p g c -> p (g c)").rearrange("p (g h k) -> p g h k", h=H, k=H)
            other = g_sig[:, :, :].unsqueeze(2).broadcast_to([P, G, H, H])
            own = g_sig[:, :, :].unsqueeze(3).broadcast_to([P, G, H, H])
            dve.wait_ge(xn_turned, G)
            dve.tensor_tensor(ahead, other, own, ALU.is_gt).then_inc(gate_step, 1)
            dve.tensor_tensor(tied, other, own, ALU.is_equal).then_inc(gate_step, 1)
            dve.wait_ge(gate_step, 4)
            dve.wait_ge(consts_done, 4)
            dve.tensor_tensor(tied, tied, before[:, :, :].unsqueeze(1).broadcast_to([P, G, H, H]), ALU.mult).then_inc(gate_step, 1)
            dve.wait_ge(gate_step, 5)
            dve.tensor_tensor(ahead, ahead, tied, ALU.add).then_inc(gate_step, 1)
            dve.wait_ge(gate_step, 6)
            dve.reduce_sum(g_rank[:, :, :], ahead, AX.X).then_inc(gate_step, 1)
            dve.wait_ge(gate_step, 7)
            dve.tensor_scalar(g_rank[:, :, :], g_rank[:, :, :], float(TOP_K), None, ALU.is_lt).then_inc(gate_step, 1)
            dve.wait_ge(gate_step, 8)
            dve.tensor_tensor(g_keep[:, :, :], g_rank[:, :, :], g_sig[:, :, :], ALU.mult).then_inc(gate_step, 1)
            dve.tensor_tensor(g_unit[:, :].rearrange("p (h b t) -> p b t h", b=B, t=NT),
                              g_rank[:, :, :].rearrange("p (b t) h -> p b t h", b=B),
                              g_sig[:, :, :].rearrange("p (b t) h -> p b t h", b=B), ALU.mult).then_inc(gate_step, 1)
            for t in range(NT):
                find_max(0, 0, t)
            split_max(0)
            for g in range(G):
                dve.wait_ge(bias_done, g + 1)
                dve.tensor_tensor(x_sb[:, g, :], bank(g % 4)[:, 0:C], x_sb[:, g, :], ALU.add).then_inc(base_done, 1)

            def low_part(n, t):
                dve.wait_ge(hi_done, n + 1)
                if not (isinstance(n, int) and n < 2):
                    dve.wait_ge(pv_done, n - 1)
                dve.tensor_tensor(prob_lo[:, t % 2, :], prob[:, t % 2, :], prob_hi[:, t % NPH, :], ALU.subtract).then_inc(lo_done, 1)

            def weigh(w):
                dve.wait_ge(den_moved, 16 * (w + 1))
                dve.reciprocal(rden[:, :], den[:, :]).then_inc(rden_done, 1)
                dve.wait_ge(rden_done, w + 1)
                dve.wait_ge(gate_fetched, 16 * (w + 1))
                if not (isinstance(w, int) and w == 0):
                    dve.wait_ge(weight_stored, 16 * w)
                dve.tensor_tensor(weight[:, :], rden[:, :], gate[:, :], ALU.mult).then_inc(weight_done, 1)

            def head(h, first=False, last=False):
                for b in range(B):
                    u = unit(h, b)
                    more = not (last and b == B - 1)
                    for t in range(NT):
                        m = 2 * (t - MAX_SLOTS[0])
                        if t in MAX_SLOTS and more:
                            find_max(u + 1, (b + 1) % B, m)
                        if t == 6 and more:
                            split_max(u + 1)
                        if not (first and b == 0 and t == 0):
                            low_part(NT * u + t - 1, (t - 1) % NT)
                        if t in MAX_SLOTS and more:
                            find_max(u + 1, (b + 1) % B, m + 1)
                        if t == 3 and not (first and b == 0):
                            weigh(u - 1)
                        if t == 7 and not last:
                            keep_qk_lo(u + 2)

            head(0, first=True)
            with dve.Fori(1, H - 1) as h:
                head(h)
            head(H - 1, last=True)
            low_part(NT * U - 1, NT - 1)
            dve.wait_ge(wo_split, 1)
            dve.tensor_tensor(wo_lo[:, :, :], wo_raw[:, :, :], wo_hi[:, :, :], ALU.subtract).then_inc(wo_split, 1)
            weigh(U - 1)
            dve.wait_ge(base_fetched, 16)
            for g in range(G):
                dve.wait_ge(proj_done, g + 1)
                dve.tensor_tensor(base[:, g, :], bank(g % 4)[:, 0:C], base[:, g, :], ALU.add).then_inc(final_done, 1)

        @block.tensor
        def _(pe):
            pe.wait_ge(consts_done, 4)
            pe.wait_ge(ctx_landed, 16 * 7)
            for cc in range(CC):
                pe.transpose(psO[:, cc * P:(cc + 1) * P], ctx_sb[:, cc * P:(cc + 1) * P], ident[:, :])
            for ps, w_sb in ((psO[:, HALF:2 * HALF], wk_sb), (psM[:, 0:HALF], wv_sb)):
                for cc in range(CC):
                    for dd in range(CC):
                        mm = pe.transpose(ps[:, cc * C + dd * P:cc * C + (dd + 1) * P],
                                          w_sb[:, dd, cc * P:(cc + 1) * P], ident[:, :])
            mm.then_inc(ctx_turned, 1)
            pe.wait_ge(ctx_kept, 3)
            for dd in range(CC):
                for cc in range(CC):
                    pe.matmul(psO[:, dd * P:(dd + 1) * P], wkT[:, cc, dd * P:(dd + 1) * P], ctxT[:, cc, :],
                              start=(cc == 0), stop=False)
                pe.matmul(psO[:, dd * P:(dd + 1) * P], bk_sb[:, dd * P:(dd + 1) * P], ones_row[:, :],
                          start=False, stop=True)
                pe.matmul(psM[:, HALF + dd:HALF + dd + 1], bq_sb[:, dd * P:(dd + 1) * P], ones_row[:, 0:1],
                          start=True, stop=True)
            for cc in range(CC):
                pe.matmul(psO[:, HALF:HALF + C], ctxT[:, cc, :], wvT[:, cc, :], start=(cc == 0), stop=False)
            pe.matmul(psO[:, HALF:HALF + C], ones_row[:, :], bv_sb[:, :], start=False, stop=True).then_inc(kv1_done, 1)
            pe.wait_ge(kv1_kept, 4)
            for cc in range(CC):
                for dd in range(CC):
                    pe.matmul(psM[:, cc * P:(cc + 1) * P], wq_sb[:, dd, cc * P:(cc + 1) * P], kT1[:, dd, :],
                              start=(dd == 0), stop=(dd == CC - 1))
            for dd in range(CC):
                mm = pe.matmul(psM[0:1, HALF:HALF + P], bq_col[:, dd:dd + 1], kT1[:, dd, :],
                               start=(dd == 0), stop=(dd == CC - 1))
            mm.then_inc(fold_done, 1)

            def turn_xn(n, k):
                pe.wait_ge(xn_done, G * n + 2 * k + 2)
                for j in range(2):
                    for cc in range(CC):
                        mm = pe.transpose(bank(k % 4)[:, (j * CC + cc) * P:(j * CC + cc + 1) * P],
                                          xn[:, 2 * k + j, cc * P:(cc + 1) * P], ident[:, :])
                mm.then_inc(xn_turned, 1)

            for k in range(G // 2):
                if k >= 4:
                    pe.wait_ge(xnT_kept, k - 3)
                turn_xn(0, k)
            pe.wait_ge(fold_kept, 2)
            pe.wait_ge(xnT_kept, G // 2)
            for j in range(G):
                t, b = divmod(j, B)
                g = b * NT + t
                dst = psM[:, j * KEYS:(j + 1) * KEYS]
                for cc in range(CC):
                    pe.matmul(dst, xnT[:, cc, g * P:(g + 1) * P], foldT[:, cc, b * KEYS:(b + 1) * KEYS],
                              start=(cc == 0), stop=False)
                mm = pe.matmul(dst, ones_row[:, :], fold_b[:, b * KEYS:(b + 1) * KEYS], start=False, stop=True)
            mm.then_inc(sc1_done, 1)
            pe.wait_ge(exp1_done, 1)
            for t in range(NT):
                mm = pe.transpose(psS[:, 0, t * P:(t + 1) * P], prob1[:, t, :], ident[:, :])
            mm.then_inc(prob1_turned, 1)
            pe.wait_ge(probT_kept, 1)
            for j in range(G):
                t, b = divmod(j, B)
                if j >= 4:
                    pe.wait_ge(x1_done, j - 3)
                dst = bank(2 + j % 4) if j % 4 < 2 else psO[:, (j % 4 - 2) * HALF:(j % 4 - 1) * HALF]
                pe.matmul(dst[:, 0:C], probT[b * KEYS:(b + 1) * KEYS, t, :], v1[b * KEYS:(b + 1) * KEYS, :],
                          start=True, stop=True).then_inc(out1_done, 1)
            for k in range(G // 2):
                if k >= 4:
                    pe.wait_ge(xT_lo_kept, k - 3)
                turn_xn(1, k)

            def project(z, b):
                for n, (w, xT) in enumerate(((wqk_hi, xT_hi), (wqk_hi, xT_lo), (wqk_lo, xT_hi))):
                    for cc in range(CC):
                        for half in range(NH):
                            mm = pe.matmul(psM[:, half * HALF:(half + 1) * HALF], w[:, cc, :],
                                           xT[:, cc, b * T + half * HALF:b * T + (half + 1) * HALF],
                                           start=(n == 0 and cc == 0), stop=(n == 2 and cc == CC - 1))
                mm.then_inc(qk_done, 1)

            def max_tile(v, b, t):
                for half in range(NH):
                    mm = pe.matmul(psM[:, half * HALF:(half + 1) * HALF], qq[b][:, t * P:(t + 1) * P],
                                   kk[b][:, half * HALF:(half + 1) * HALF], start=True, stop=True)
                mm.then_inc(max_scores, 1)

            def turn_max(v, b):
                pe.wait_ge(max_found, NT * (v + 1))
                pe.transpose(psM[0:NT, 0:P], row_max[:, b, :], ident[:, :]).then_inc(max_turned, 1)

            pe.wait_ge(xT_hi_kept, G // 2)
            pe.wait_ge(xT_lo_kept, G // 2)
            pe.wait_ge(wqk_split, 2)
            project(0, 0)
            pe.wait_ge(wv_split, 2)
            for g in range(G):
                if g >= 4:
                    pe.wait_ge(v_kept, g - 3)
                terms = ((xT_hi, wv_hi), (xT_hi, wv_lo), (xT_lo, wv_hi))
                for n, (xT, w) in enumerate(terms):
                    for cc in range(CC):
                        mm = pe.matmul(bank(g % 4), xT[:, cc, g * P:(g + 1) * P], w[:, cc, :],
                                       start=(n == 0 and cc == 0), stop=(n == 2 and cc == CC - 1))
                mm.then_inc(v_done, 1)
                if g == 3:
                    pe.wait_ge(qk_hi_kept, 1)
                    pe.wait_ge(qk_lo_kept, 1)
                    project(1, 1)
            pe.wait_ge(v_kept, G)
            pe.wait_ge(ws_split, 2)
            for c in range(4):
                for n, (w, xT) in enumerate(((ws_hi, xT_hi), (ws_hi, xT_lo), (ws_lo, xT_hi))):
                    for cc in range(CC):
                        mm = pe.matmul(bank(c)[0:H, :], w[:, cc, :], xT[:, cc, c * HALF:(c + 1) * HALF],
                                       start=(n == 0 and cc == 0), stop=(n == 2 and cc == CC - 1))
                mm.then_inc(logits_done, 1)
            pe.wait_ge(logits_kept, 4)
            for g in range(G):
                mm = pe.transpose(psO[:, g * H:(g + 1) * H], sT_raw[:, g * P:(g + 1) * P], ident[0:H, 0:H])
            mm.then_inc(logits_turned, 1)
            pe.wait_ge(qk_hi_kept, 2)
            pe.wait_ge(qk_lo_kept, 2)
            pe.wait_ge(pairs_set, 64)
            for t in range(NT):
                if t > 0:
                    pe.wait_ge(max_found, t)
                max_tile(0, 0, t)
            turn_max(0, 0)
            pe.wait_ge(gate_step, 10)
            for g in range(G):
                pe.transpose(bank(g // 4)[0:H, (g % 4) * P:(g % 4 + 1) * P], g_keep[:, g, :], ident[:, :])
            pe.transpose(psO[:, HALF:HALF + P], g_unit[:, :], ident[:, :]).then_inc(gate_turned, 1)
            pe.wait_ge(gate_kept, 2)
            for g in range(G):
                if g >= 4:
                    pe.wait_ge(base_done, g - 3)
                pe.matmul(bank(g % 4)[:, 0:C], sT[:, g * P:(g + 1) * P], bo_sb[:, :], start=True, stop=True).then_inc(bias_done, 1)
            pe.wait_ge(base_done, G)

            def score_tile(u, b, t, first):
                if t == 0:
                    pe.wait_ge(pairs_set, 64 * (u + 1))
                    pe.wait_ge(rest_set, 32 * (u + 1))
                if not (first and t < 2):
                    pe.wait_ge(exp_done, NT * u + t - 1)
                for half in range(NH):
                    pe.matmul(psS[:, t % 2, half * HALF:(half + 1) * HALF], kk[b][:, t * P:(t + 1) * P],
                              qq[b][:, half * HALF:(half + 1) * HALF], start=True, stop=False)
                if t == 0:
                    pe.wait_ge(max_set, 32 * (u + 1))
                for half in range(NH):
                    mm = pe.matmul(psS[:, t % 2, half * HALF:(half + 1) * HALF], k1[b][:, t * P:(t + 1) * P],
                                   qm[b][:, half * HALF:(half + 1) * HALF], start=False, stop=True)
                mm.then_inc(scores_done, 1)

            def pv_tile(w, b, t):
                if t == 0:
                    pe.wait_ge(v_split, 2 * (w + 1))
                    if not (isinstance(w, int) and w == 0):
                        pe.wait_ge(num_kept, w)
                pe.wait_ge(lo_done, NT * w + t + 1)
                hi, lo = prob_hi[:, t % NPH, :], prob_lo[:, t % 2, :]
                with_ones, v_lo = v_st[b][:, t, 0:DH + 2], v_st[b][:, t, VLO:VLO + DH]
                for half in range(NH):
                    pe.matmul(psO[0:DH + 2, half * HALF:(half + 1) * HALF], with_ones,
                              hi[:, half * HALF:(half + 1) * HALF], start=(t == 0), stop=False)
                for half in range(NH):
                    mm = pe.matmul(psO[0:DH, half * HALF:(half + 1) * HALF], v_lo,
                                   hi[:, half * HALF:(half + 1) * HALF], start=False, stop=False)
                if t == NT - 1 - LAG:
                    mm.then_inc(stacks_free, 1)
                for half in range(NH):
                    mm = pe.matmul(psO[0:DH + 2, half * HALF:(half + 1) * HALF], with_ones,
                                   lo[:, half * HALF:(half + 1) * HALF], start=False, stop=(t == NT - 1))
                mm.then_inc(pv_done, 1)

            def head(h, first=False, last=False):
                for b in range(B):
                    u = unit(h, b)
                    more = not (last and b == B - 1)
                    for t in range(NT):
                        m = 2 * (t - MAX_SLOTS[0])
                        if t in MAX_SLOTS and more:
                            if m == 0:
                                pe.wait_ge(pairs_set, 64 * (u + 2))
                                pe.wait_ge(qk_hi_kept, u + 2)
                                pe.wait_ge(qk_lo_kept, u + 2)
                            else:
                                pe.wait_ge(max_found, NT * (u + 1) + m)
                            max_tile(u + 1, (b + 1) % B, m)
                        score_tile(u, b, t, first and b == 0)
                        if t in MAX_SLOTS and more:
                            pe.wait_ge(max_found, NT * (u + 1) + m + 1)
                            max_tile(u + 1, (b + 1) % B, m + 1)
                        if t == 6 and more:
                            turn_max(u + 1, (b + 1) % B)
                        if t >= LAG:
                            pv_tile(u, b, t - LAG)
                        elif not (first and b == 0):
                            pv_tile(u - 1, (b + 1) % B, NT - LAG + t)
                        if t == 6 and not last:
                            pe.wait_ge(max_split, 2 * (u + 2))
                            if b == 0:
                                pe.wait_ge(wqk_split, 2 * (h + 2))
                            project(u + 2, b)

            head(0, first=True)
            with pe.Fori(1, H - 1) as h:
                head(h)
            head(H - 1, last=True)
            for t in range(NT - LAG, NT):
                pv_tile(U - 1, B - 1, t)
            pe.wait_ge(wo_split, 2)
            pe.wait_ge(o_set, 32 * U)
            for g in range(G):
                if g >= 4:
                    pe.wait_ge(final_done, g - 3)
                b, t = divmod(g, NT)
                for h in range(H):
                    for w in (wo_hi, wo_lo):
                        mm = pe.matmul(bank(g % 4)[:, 0:C], o_st[:, b, h, t * P:(t + 1) * P], w[:, h, :],
                                       start=(h == 0 and w is wo_hi), stop=(h == H - 1 and w is wo_lo))
                mm.then_inc(proj_done, 1)


_INS = ['x', 'ctx_1024', 'L0_xattn_Wq', 'L0_xattn_bq', 'L0_xattn_Wk', 'L0_xattn_bk', 'L0_xattn_Wv',
        'L0_xattn_bv', 'L0_ffn_Wq', 'L0_ffn_Wkv', 'L0_ffn_Ws', 'L0_ffn_Wo', 'L0_ffn_bo']


def kernel(**inputs):
    import numpy as _np
    import concourse.bacc as _bacc
    from concourse import mybir as _mybir
    from concourse.bass_utils import run_bass_kernel_spmd as _run

    nc = _bacc.Bacc("TRN2", target_bir_lowering=False, num_devices=1)
    arrays, args = {}, []
    for name in _INS:
        a = _np.ascontiguousarray(inputs[name])
        arrays[f"in_{name}_dram"] = a
        args.append(nc.dram_tensor(f"in_{name}_dram", a.shape, _mybir.dt.from_np(a.dtype), kind="ExternalInput").ap())
    shape = inputs['x'].shape
    args.append(nc.dram_tensor("out_0_dram", shape, _mybir.dt.from_np(_np.dtype("float32")), kind="ExternalOutput").ap())
    build(nc, *args)
    r = _run(nc, [arrays], core_ids=[0])
    return r.results[0]["out_0_dram"]
```

```python
from contextlib import ExitStack

import concourse.bass as bass
from concourse import mybir

P = 128
F32 = mybir.dt.float32
F32R = mybir.dt.float32r
ALU = mybir.AluOpType
ACT = mybir.ActivationFunctionType
AX = mybir.AxisListType

LN_EPS = 1e-5
TOP_K = 3


def build(nc, x, ctx_in, wq1, bq1, wk1, bk1, wv1, bv1, wq2, wkv2, ws2, wo2, bo2, out):
    B, T, C = x.shape
    KEYS = ctx_in.shape[1]
    H, DH, _ = wo2.shape
    HD = H * DH
    CC = C // P
    NT = T // P
    G = B * NT
    U = B * H
    SCALE = float(DH) ** -0.5
    HALF = 512
    NH = T // HALF
    ONES = DH
    VLO = DH + 2
    VW = 2 * DH + 2
    NPH = 4
    LAG = 2
    FIRST_MAX, GATES_AT, GATES_BACK_AT = 6, 8, 5
    WEIGH_AT = 0
    WL = 16
    WR = T // WL
    assert B == 2 and C == CC * P and B * KEYS == P and 2 * DH == P and U * NT == P and NT == 8

    base_d = nc.dram_tensor("base_d", (P, G, C), F32, kind="Internal").ap()
    v_d = nc.dram_tensor("v_d", (B, H, P, NT * DH), F32, kind="Internal").ap()
    gate_d = nc.dram_tensor("gate_d", (P, P), F32, kind="Internal").ap()
    weight_d = nc.dram_tensor("weight_d", (B, T), F32, kind="Internal").ap()

    with ExitStack() as top:
        sem_names = {}

        def sem(name):
            sem_names[name] = top.enter_context(nc.semaphore(name))
            return sem_names[name]

        def sb(name, shape, dt=F32, stack=top):
            return stack.enter_context(nc.sbuf_tensor(name, shape, dt))

        ident = sb("ident", [P, P])
        ones_row = sb("ones_row", [1, P])
        zero = sb("zero", [P, 1])
        wqk_raw = sb("wqk_raw", [P, CC, P])
        wqk_hi = sb("wqk_hi", [P, CC, P], F32R)
        wqk_lo = sb("wqk_lo", [P, CC, P], F32R)
        ws_raw = sb("ws_raw", [P, CC, H])
        ws_hi = sb("ws_hi", [P, CC, H], F32R)
        ws_lo = sb("ws_lo", [P, CC, H], F32R)
        qk_hi = [sb(f"qk_hi{b}", [P, T], F32R) for b in range(B)]
        qk_lo = [sb(f"qk_lo{b}", [P, T], F32R) for b in range(B)]
        stacks0 = [sb(f"{n}0", [P, T], F32R) for n in ("kk", "qq", "k1", "qm")]
        v_raw = sb("v_raw", [P, NT, DH])
        v_st = [sb(f"v_st{b}", [P, NT, VW], F32R) for b in range(B)]
        row_max = sb("row_max", [P, B, NT])
        neg_max = sb("neg_max", [NT, 2, P], F32R)
        den = sb("den", [WR, WL])
        rden = sb("rden", [WR, WL])
        gate = sb("gate", [WR, WL])
        weight = sb("weight", [WR, WL])

        def overlay(*stages):
            widest, got = 0, []
            for named in stages:
                size = sum(w * 4 for _, w in ((n, _width(s)) for n, s, _ in named))
                widest = max(widest, size)
                with ExitStack() as own:
                    got.append([sb(n, s, d, own) for n, s, d in named])
            sb(f"room{len(rooms)}", [P, widest // 4])
            rooms.append(widest)
            return got

        def _width(shape):
            n = 1
            for s in shape[1:]:
                n *= s
            return n

        rooms = []
        (wv_raw, wv_hi, wv_lo), stacks1 = overlay(
            [("wv_raw", [P, CC, HD], F32), ("wv_hi", [P, CC, HD], F32R), ("wv_lo", [P, CC, HD], F32R)],
            [(f"{n}1", [P, T], F32R) for n in ("kk", "qq", "k1", "qm")])
        kk, qq, k1, qm = zip(stacks0, stacks1)
        (xT_hi, xT_lo), (wo_raw, wo_hi, wo_lo, base0) = overlay(
            [("xT_hi", [P, CC, B * T], F32R), ("xT_lo", [P, CC, B * T], F32R)],
            [("wo_raw", [P, H, C], F32), ("wo_hi", [P, H, C], F32R), ("wo_lo", [P, H, C], F32R),
             ("base0", [P, NT, C], F32)])
        (x_sb, xn, xnT, logits, gate_st), (o_st,) = overlay(
            [("x_sb", [P, G, C], F32), ("xn", [P, G, C], F32), ("xnT", [P, CC, B * T], F32),
             ("logits", [H, B * T], F32), ("gate_st", [P, B * T], F32R)],
            [("o_st", [P, B, H, T], F32R)])
        (ctx_sb, ctxT, wk_sb, wv_sb, wq_sb, wkT, wvT, kT1, foldT, fold_b, v1, prob1, probT,
         bk_sb, bq_sb, bq_col, bv_sb, bo_raw, bo_hi, bo_lo, shift,
         stats, mean_var, rstd, mx1, sum1, rsum1, g_exp, g_sig, g_rank, g_unit, g_unitT, before), \
            (prob, prob_hi, prob_lo, num, wide, o_hi), (base1,) = overlay(
            [("ctx_sb", [P, C], F32), ("ctxT", [P, CC, P], F32), ("wk_sb", [P, CC, C], F32),
             ("wv_sb", [P, CC, C], F32), ("wq_sb", [P, CC, C], F32), ("wkT", [P, CC, C], F32),
             ("wvT", [P, CC, C], F32), ("kT1", [P, CC, P], F32), ("foldT", [P, CC, P], F32),
             ("fold_b", [1, P], F32), ("v1", [P, B, 2, C], F32), 
             ("prob1", [P, B, NT * KEYS], F32), ("probT", [P, B, NT * KEYS], F32), ("bk_sb", [1, C], F32),
             ("bq_sb", [1, C], F32), ("bq_col", [P, CC], F32), ("bv_sb", [1, C], F32), ("bo_raw", [P, C], F32), ("bo_hi", [P, C], F32R),
             ("bo_lo", [P, C], F32R),
             ("shift", [P, G], F32),
             ("stats", [P, G, 6], F32), ("mean_var", [P, G, 2], F32), ("rstd", [P, G], F32),
             ("mx1", [P, G], F32), ("sum1", [P, G], F32), ("rsum1", [P, G], F32),
             ("g_exp", [P, G, H], F32), ("g_sig", [P, G, H], F32), ("g_rank", [P, G, H], F32),
             ("g_unit", [P, P], F32), ("g_unitT", [P, P], F32), ("before", [P, H, H], F32)],
            [("prob", [P, 2, T], F32), ("prob_hi", [P, NPH, T], F32R),
             ("prob_lo", [P, 2, T], F32R), ("num", [DH + 1, T], F32), ("wide", [DH, T], F32),
             ("o_hi", [DH, T], F32R)],
            [("base1", [P, NT, C], F32)])

        STAGES = 4
        v_stage = xnT[:, :, :].rearrange("p c n -> p (c n)").rearrange("p (s h t d) -> p s h t d", s=STAGES, h=H, t=2)

        psS = top.enter_context(nc.psum_tensor("psS", [P, 2, T], F32))
        psM = top.enter_context(nc.psum_tensor("psM", [P, T], F32))
        psO = top.enter_context(nc.psum_tensor("psO", [P, T], F32))

        def bank(n):
            return psS[:, n // 2, (n % 2) * HALF:(n % 2 + 1) * HALF]

        def pair_bank(g):
            r = g // 2 % 4
            whole = bank(2 + r) if r < 2 else psO[:, (r - 2) * HALF:(r - 1) * HALF]
            return whole[:, g % 2 * C:(g % 2 + 1) * C]

        def final_half(g):
            if g < NT:
                return psM[:, (g % 2) * HALF:(g % 2) * HALF + C]
            banks = (bank(0), bank(1), bank(2), bank(3), psO[:, 0:HALF], psO[:, HALF:2 * HALF], psM[:, 0:HALF], psM[:, HALF:2 * HALF])
            return banks[g - NT][:, 0:C]

        x_in = [sem(f"x_in{i}") for i in range(4)]
        ctx_landed = sem("ctx_landed")
        wqk_landed = sem("wqk_landed")
        wv_landed = sem("wv_landed")
        small_landed = sem("small_landed")
        consts_set = sem("consts_set")
        consts_done = sem("consts_done")
        stats_done = sem("stats_done")
        var_done = sem("var_done")
        eps_added = sem("eps_added")
        std_done = sem("std_done")
        rstd_done = sem("rstd_done")
        xn_done = sem("xn_done")
        shift_done = sem("shift_done")
        xn2_done = sem("xn2_done")
        ctx_turned = sem("ctx_turned")
        ctx_kept = sem("ctx_kept")
        kv1_done = sem("kv1_done")
        kv1_kept = sem("kv1_kept")
        fold_done = sem("fold_done")
        fold_kept = sem("fold_kept")
        xn_turned = sem("xn_turned")
        xnT_kept = sem("xnT_kept")
        xT_hi_kept = sem("xT_hi_kept")
        xT_lo_kept = sem("xT_lo_kept")
        sc1_done = sem("sc1_done")
        max1_done = sem("max1_done")
        sub1_done = sem("sub1_done")
        exp1_done = sem("exp1_done")
        sum1_done = sem("sum1_done")
        rsum1_done = sem("rsum1_done")
        prob1_turned = sem("prob1_turned")
        probT_kept = sem("probT_kept")
        out1_done = sem("out1_done")
        x1_done = sem("x1_done")
        wv_split = sem("wv_split")
        v_done = sem("v_done")
        v_kept = sem("v_kept")
        v_stored = [sem(f"v_stored{i}") for i in range(STAGES)]
        ws_split = sem("ws_split")
        logits_done = sem("logits_done")
        logits_kept = sem("logits_kept")
        v1_spread = sem("v1_spread")
        bo_cleared = sem("bo_cleared")
        v1_cleared = sem("v1_cleared")
        gate_row = sem("gate_row")
        gate_split = sem("gate_split")
        gates_back = sem("gates_back")
        bo_split = sem("bo_split")
        logits_turned = sem("logits_turned")
        gate_exp = sem("gate_exp")
        gate_step = sem("gate_step")
        gate_turned = sem("gate_turned")
        gate_kept = sem("gate_kept")
        gate_stored = sem("gate_stored")
        bias_done = sem("bias_done")
        base_done = sem("base_done")
        base_stored = sem("base_stored")

        wqk_split = sem("wqk_split")
        qk_done = sem("qk_done")
        qk_hi_kept = sem("qk_hi_kept")
        qk_lo_kept = sem("qk_lo_kept")
        stacks_cleared = [sem(f"stacks_cleared{b}") for b in range(B)]
        stacks_free = sem("stacks_free")
        pairs_set = sem("pairs_set")
        rest_set = [sem(f"rest_set{b}") for b in range(B)]
        v_fetched = sem("v_fetched")
        v_split = sem("v_split")
        max_scores = sem("max_scores")
        max_found = sem("max_found")
        max_turned = sem("max_turned")
        max_split = sem("max_split")
        max_set = sem("max_set")
        scores_done = sem("scores_done")
        exp_done = sem("exp_done")
        hi_done = sem("hi_done")
        lo_done = sem("lo_done")
        pv_done = sem("pv_done")
        num_kept = sem("num_kept")
        den_moved = sem("den_moved")
        gate_fetched = sem("gate_fetched")
        rden_done = sem("rden_done")
        weight_done = sem("weight_done")
        weight_stored = sem("weight_stored")
        wide_fetched = sem("wide_fetched")
        out_split = sem("out_split")
        o_set = sem("o_set")
        last_o_set = sem("last_o_set")
        wo_landed = sem("wo_landed")
        wo_split = sem("wo_split")
        base_fetched = sem("base_fetched")
        proj_done = sem("proj_done")
        final_done = sem("final_done")
        out_stored = sem("out_stored")

        x_tiles = x.rearrange("b (t p) c -> p (b t) c", p=P)
        out_tiles = out.rearrange("b (t p) c -> p (b t) c", p=P)
        wq_heads = wq2.rearrange("(cc p) n -> p cc n", p=P)
        wkv_heads = wkv2.rearrange("(cc p) n -> p cc n", p=P)

        gate_rows = gate_d.rearrange("r (a i) -> (r a) i", i=WL)

        def unit(h, b):
            return B * h + b

        block = top.enter_context(nc.Block())

        @block.sync
        def _(sp):
            for i in range(4):
                w = G // 4
                sp.dma_start(x_sb[:, i * w:(i + 1) * w, :], x_tiles[:, i * w:(i + 1) * w, :]).then_inc(x_in[i], 16)
                if i == 0:
                    sp.dma_start(ctx_sb[:, :], ctx_in.rearrange("b k c -> (b k) c")).then_inc(ctx_landed, 16)
                    for w_sb, w_in in ((wk_sb, wk1), (wv_sb, wv1), (wq_sb, wq1)):
                        sp.dma_start(w_sb[:, :, :], w_in.rearrange("(dd p) c -> p dd c", p=P)).then_inc(ctx_landed, 16)
                    for b_sb, b_in in ((bk_sb, bk1), (bq_sb, bq1), (bv_sb, bv1)):
                        sp.dma_start(b_sb[:, :], b_in.rearrange("(a c) -> a c", a=1)).then_inc(ctx_landed, 16)
            sp.dma_start(ws_raw[:, :, :], ws2.rearrange("(cc p) h -> p cc h", p=P)).then_inc(small_landed, 16)
            sp.wait_ge(bo_cleared, 1)
            for row in (0, 32):
                sp.dma_start(bo_raw[row:row + H, :], bo2).then_inc(small_landed, 16)
            sp.dma_start(wv_raw[:, :, :], wkv_heads[:, :, HD:2 * HD]).then_inc(wv_landed, 16)

            def fetch_wqk(h):
                if not (isinstance(h, int) and h == 0):
                    sp.wait_ge(wqk_split, 2 * h)
                sp.dma_start(wqk_raw[:, :, 0:DH], wq_heads[:, :, bass.ds(h * DH, DH)]).then_inc(wqk_landed, 16)
                sp.dma_start(wqk_raw[:, :, DH:2 * DH], wkv_heads[:, :, bass.ds(h * DH, DH)]).then_inc(wqk_landed, 16)

            def stack_pairs(v, b):
                if isinstance(v, int) and v < B:
                    sp.wait_ge(stacks_cleared[b], 1)
                    sp.wait_ge(qk_lo_kept, v + 1)
                else:
                    sp.wait_ge(stacks_free, v - 1)
                hi, lo = qk_hi[b], qk_lo[b]
                for dst, src in ((kk[b][0:DH, :], hi[DH:P, :]), (kk[b][DH:P, :], hi[DH:P, :]),
                                 (qq[b][0:DH, :], hi[0:DH, :]), (qq[b][DH:P, :], lo[0:DH, :])):
                    sp.dma_start(dst.bitcast(F32), src.bitcast(F32)).then_inc(pairs_set, 16)

            def stack_rest(b):
                for dst, src in ((k1[b][0:DH, :], qk_lo[b][DH:P, :]), (qm[b][0:DH, :], qk_hi[b][0:DH, :])):
                    sp.dma_start(dst.bitcast(F32), src.bitcast(F32)).then_inc(rest_set[b], 16)

            def fetch_v(v, h, b):
                if not (isinstance(v, int) and v == 0):
                    sp.wait_ge(v_split, 2 * v)
                sp.dma_start(v_raw[:, :, :], v_d[b, bass.ds(h, 1)].rearrange("a p (t d) -> p (a t) d", d=DH)).then_inc(v_fetched, 16)

            def set_max(v, b):
                sp.wait_ge(max_split, 2 * (v + 1))
                for part in range(2):
                    sp.dma_start(qm[b][DH + part:DH + part + 1, :].bitcast(F32).rearrange("a (t p) -> a t p", p=P),
                                 neg_max[:, part, :].bitcast(F32)).then_inc(max_set, 16)

            def weigh(w, b):
                first = isinstance(w, int) and w == 0
                if not first:
                    sp.wait_ge(weight_done, w)
                sp.dma_start(gate[:, :], gate_rows[bass.ds(w * WR, WR), :]).then_inc(gate_fetched, 16)
                sp.wait_ge(num_kept, w + 1)
                sp.dma_start(den[:, :], num[DH:DH + 1, :].rearrange("a (t p) -> a t p", p=WL)).then_inc(den_moved, 16)
                sp.wait_ge(weight_done, w + 1)
                sp.dma_start(weight_d[b].rearrange("(t p) -> t p", p=WL), weight[:, :]).then_inc(weight_stored, 16)
                sp.wait_ge(weight_stored, 16 * (w + 1))
                sp.dma_start(wide[:, :], weight_d[b:b + 1, :].broadcast_to([DH, T])).then_inc(wide_fetched, 16)

            fetch_wqk(0)
            fetch_wqk(1)
            stack_pairs(0, 0)
            stack_rest(0)
            sp.wait_ge(gate_row, 1)
            sp.dma_start(gate_d, g_unitT[:, :]).then_inc(gate_stored, 16)
            sp.wait_ge(gate_stored, 16)
            sp.dma_start(logits[:, :].rearrange("h (g i) -> h g i", i=P),
                         gate_d.rearrange("(h g) i -> h g i", h=H)).then_inc(gates_back, 16)
            set_max(0, 0)
            stack_pairs(1, 1)
            for i in range(STAGES):
                sp.wait_ge(v_stored[i], 16 * (G // 2 // STAGES))
            fetch_v(0, 0, 0)
            sp.wait_ge(base_done, NT)
            sp.dma_start(base_d, x_sb[:, :, :]).then_inc(base_stored, 16)

            def head(h, first=False, last=False, ahead=True):
                for b in range(B):
                    u = unit(h, b)
                    if not (last and b == B - 1):
                        stack_rest((b + 1) % B)
                        fetch_v(u + 1, h + (b + 1) // B, (b + 1) % B)
                    if b == 0 and ahead:
                        fetch_wqk(h + 2)
                    if not (first and b == 0):
                        weigh(u - 1, (b + 1) % B)
                    if not last:
                        stack_pairs(u + 2, b)
                    if not (last and b == B - 1):
                        set_max(u + 1, (b + 1) % B)

            head(0, first=True)
            with sp.Fori(1, H - 2) as h:
                head(h)
            head(H - 2, ahead=False)
            head(H - 1, last=True, ahead=False)
            sp.wait_ge(qk_done, U)
            for part in range(2):
                sp.dma_start(wo_raw[part * DH:(part + 1) * DH, :, :], wo2.rearrange("h d c -> d h c")).then_inc(wo_landed, 16)
            sp.dma_start(base0[:, :, :], base_d[:, 0:NT, :]).then_inc(base_fetched, 16)
            sp.wait_ge(lo_done, NT * U)
            sp.dma_start(base1[:, :, :], base_d[:, NT:G, :]).then_inc(base_fetched, 16)
            weigh(U - 1, (U - 1) % B)
            sp.wait_ge(out_split, 3 * U)
            for part, src in enumerate((o_hi, num)):
                sp.dma_start(o_st[part * DH:(part + 1) * DH, B - 1, H - 1, :].bitcast(F32), src[0:DH, :].bitcast(F32)).then_inc(last_o_set, 16)
            for g in range(G):
                sp.wait_ge(final_done, g + 1)
                sp.dma_start(out_tiles[:, g, :], (base0, base1)[g // NT][:, g % NT, :]).then_inc(out_stored, 16)
            sp.wait_ge(out_stored, 16 * G)

        @block.gpsimd
        def _(pool):
            nc.gpsimd.memset(ident[:, :], 0.0).then_inc(consts_set, 1)
            nc.gpsimd.memset(ones_row[:, :], 1.0).then_inc(consts_done, 1)
            nc.gpsimd.memset(before[:, :, :], 1.0).then_inc(consts_set, 1)
            nc.gpsimd.memset(zero[:, :], 0.0).then_inc(consts_set, 1)
            pool.wait_ge(consts_set, 3)
            nc.gpsimd.affine_select(out=ident[:, :], in_=ident[:, :], compare_op=ALU.not_equal, fill=1.0,
                                    base=0, pattern=[[-1, P]], channel_multiplier=1).then_inc(consts_done, 1)
            nc.gpsimd.affine_select(out=before[:, :, :], in_=before[:, :, :], compare_op=ALU.is_gt, fill=0.0,
                                    base=0, pattern=[[1, H], [-1, H]], channel_multiplier=0).then_inc(consts_done, 1)
            for b in range(B):
                last = nc.gpsimd.memset(v_st[b][:, :, ONES:ONES + 2].bitcast(F32), 1.0)
            last.then_inc(consts_done, 1)

            def round_to(dst, src):
                return nc.gpsimd.tensor_tensor(dst, src, zero[:, :].unsqueeze(2).broadcast_to(src.shape), ALU.add)

            def split_wqk(h):
                pool.wait_ge(wqk_landed, 32 * (h + 1))
                if not (isinstance(h, int) and h == 0):
                    pool.wait_ge(qk_done, B * h)
                round_to(wqk_hi[:, :, :], wqk_raw[:, :, :]).then_inc(wqk_split, 1)
                pool.wait_ge(wqk_split, 2 * h + 1)
                nc.gpsimd.tensor_tensor(wqk_lo[:, :, :], wqk_raw[:, :, :], wqk_hi[:, :, :], ALU.subtract).then_inc(wqk_split, 1)

            def split_v(v, b):
                pool.wait_ge(v_fetched, 16 * (v + 1))
                if not (isinstance(v, int) and v < B):
                    pool.wait_ge(pv_done, NT * (v - 1))
                round_to(v_st[b][:, :, 0:DH], v_raw[:, :, :]).then_inc(v_split, 1)
                pool.wait_ge(v_split, 2 * v + 1)
                nc.gpsimd.tensor_tensor(v_st[b][:, :, VLO:VLO + DH], v_raw[:, :, :], v_st[b][:, :, 0:DH],
                                        ALU.subtract).then_inc(v_split, 1)

            def finish(w, h, b):
                pool.wait_ge(wide_fetched, 16 * (w + 1))
                if not (isinstance(w, int) and w == 0):
                    pool.wait_ge(o_set, 32 * w)
                nc.gpsimd.tensor_tensor(o_hi[:, :], num[0:DH, :], wide[:, :], ALU.mult).then_inc(out_split, 1)
                pool.wait_ge(out_split, 3 * w + 1)
                nc.gpsimd.tensor_tensor(num[0:DH, :], num[0:DH, :], wide[:, :], ALU.mult).then_inc(out_split, 1)
                pool.wait_ge(out_split, 3 * w + 2)
                nc.gpsimd.tensor_tensor(num[0:DH, :], num[0:DH, :], o_hi[:, :], ALU.subtract).then_inc(out_split, 1)
                if isinstance(w, int) and w == 0:
                    pool.wait_ge(base_stored, 16)
                pool.wait_ge(out_split, 3 * w + 3)
                for part, src in enumerate((o_hi, num)):
                    pool.dma_start(o_st[part * DH:(part + 1) * DH, b, bass.ds(h, 1), :].bitcast(F32).rearrange("p a t -> p (a t)"),
                                   src[0:DH, :].bitcast(F32)).then_inc(o_set, 16)

            def store_v(r):
                pool.wait_ge(v_kept, 2 * r + 2)
                b, t = divmod(2 * r, NT)
                pool.dma_start(v_d[b, :, :, t * DH:(t + 2) * DH].rearrange("h p n -> p h n"),
                               v_stage[:, r % STAGES].rearrange("p h t d -> p h (t d)")).then_inc(v_stored[r % STAGES], 16)

            nc.gpsimd.memset(bo_raw[:, :], 0.0).then_inc(bo_cleared, 1)
            split_wqk(0)
            pool.wait_ge(small_landed, 48)
            nc.gpsimd.tensor_tensor(ws_hi[:, :, :], ws_raw[:, :, :], zero[:, :].unsqueeze(2).broadcast_to([P, CC, H]),
                                    ALU.add).then_inc(ws_split, 1)
            pool.wait_ge(ws_split, 1)
            nc.gpsimd.tensor_tensor(ws_lo[:, :, :], ws_raw[:, :, :], ws_hi[:, :, :], ALU.subtract).then_inc(ws_split, 1)
            pool.wait_ge(wv_landed, 16)
            round_to(wv_hi[:, :, :], wv_raw[:, :, :]).then_inc(wv_split, 1)
            pool.wait_ge(wv_split, 1)
            nc.gpsimd.tensor_tensor(wv_lo[:, :, :], wv_raw[:, :, :], wv_hi[:, :, :], ALU.subtract).then_inc(wv_split, 1)
            nc.gpsimd.tensor_copy(bo_hi[:, :], bo_raw[:, :]).then_inc(bo_split, 1)
            pool.wait_ge(bo_split, 1)
            nc.gpsimd.tensor_tensor(bo_lo[:, :], bo_raw[:, :], bo_hi[:, :], ALU.subtract).then_inc(bo_split, 1)
            nc.gpsimd.memset(gate_st[:, :].bitcast(F32), 0.0).then_inc(bo_split, 1)
            split_wqk(1)
            for r in range(G // 2):
                store_v(r)
            pool.wait_ge(v_done, G)
            pool.wait_ge(wqk_split, 4)
            nc.gpsimd.memset(k1[1][DH:P, :].bitcast(F32), 1.0)
            nc.gpsimd.memset(qm[1][DH:P, :].bitcast(F32), 0.0).then_inc(stacks_cleared[1], 1)
            pool.wait_ge(stacks_cleared[1], 1)
            split_v(0, 0)

            def head(h, first=False, last=False, ahead=True):
                for b in range(B):
                    u = unit(h, b)
                    if b == B - 1 and ahead:
                        split_wqk(h + 2)
                    if not (last and b == B - 1):
                        split_v(u + 1, (b + 1) % B)
                    if not (first and b == 0):
                        finish(u - 1, h if b else h - 1, (b + 1) % B)

            head(0, first=True)
            with pool.Fori(1, H - 2) as h:
                head(h)
            head(H - 2, ahead=False)
            head(H - 1, last=True, ahead=False)

        @block.scalar
        def _(act):
            act.wait_ge(ctx_turned, 1)
            act.copy(ctxT[:, :, :], psO[:, 0:C]).then_inc(ctx_kept, 1)
            act.copy(wkT[:, :, :], psO[:, HALF:HALF + CC * C]).then_inc(ctx_kept, 1)
            act.copy(wvT[:, :, :], psM[:, 0:CC * C]).then_inc(ctx_kept, 1)

            def std(n):
                act.wait_ge(eps_added, n + 1)
                part = rstd[:, (n % B) * NT:(n % B + 1) * NT]
                act.activation(part, part, ACT.Sqrt).then_inc(std_done, 1)

            std(0)
            std(1)
            act.wait_ge(kv1_done, 1)
            act.copy(kT1[:, :, :], psO[:, 0:C]).then_inc(kv1_kept, 1)
            act.copy(bq_col[:, :], psM[:, HALF:HALF + CC]).then_inc(kv1_kept, 1)
            act.wait_ge(v1_cleared, 1)
            for b in range(B):
                for odd in range(2):
                    act.copy(v1[odd * KEYS:(odd + 1) * KEYS, b, odd, :],
                             psO[b * KEYS:(b + 1) * KEYS, HALF:HALF + C]).then_inc(v1_spread, 1)

            def norm_half(n):
                act.wait_ge(shift_done, n - B + 1)
                for g in range(n % B * NT, (n % B + 1) * NT):
                    act.activation(xn[:, g, :], x_sb[:, g, :], ACT.Identity, bias=shift[:, g:g + 1],
                                   scale=rstd[:, g:g + 1]).then_inc(xn2_done, 1)

            def keep_xnT(k):
                act.wait_ge(xn_turned, k + 1)
                act.copy(xnT[:, :, 2 * k * P:(2 * k + 2) * P].rearrange("p c (g q) -> p g c q", q=P),
                         bank(k % 4).rearrange("p (g c q) -> p g c q", g=2, c=CC)).then_inc(xnT_kept, 1)

            def keep_xT_hi(k):
                act.wait_ge(xn_turned, G // 2 + k + 1)
                act.copy(xT_hi[:, :, 2 * k * P:(2 * k + 2) * P].rearrange("p c (g q) -> p g c q", q=P),
                         bank(k % 4).rearrange("p (g c q) -> p g c q", g=2, c=CC)).then_inc(xT_hi_kept, 1)

            for k in range(2):
                keep_xnT(k)
            act.wait_ge(fold_done, 1)
            act.copy(foldT[:, :, :], psM[:, 0:C]).then_inc(fold_kept, 1)
            act.copy(fold_b[:, :], psM[0:1, HALF:HALF + P]).then_inc(fold_kept, 1)
            for k in range(2, G // 2):
                keep_xnT(k)
            for b in range(B):
                act.wait_ge(sub1_done, b + 1)
                act.activation(prob1[:, b, :], prob1[:, b, :], ACT.Exp).then_inc(exp1_done, 1)
                act.wait_ge(prob1_turned, b + 1)
                act.copy(probT[:, b, :], bank(b)).then_inc(probT_kept, 1)

            def keep_qk_hi(z, b):
                act.wait_ge(qk_done, z + 1)
                act.copy(qk_hi[b][:, :], psM[:, :]).then_inc(qk_hi_kept, 1)

            std(2)
            norm_half(2)
            for k in range(G // 4):
                keep_xT_hi(k)
            std(3)
            norm_half(3)
            keep_qk_hi(0, 0)
            for k in range(G // 4, G // 2):
                keep_xT_hi(k)
            keep_qk_hi(1, 1)
            for c in range(4):
                act.wait_ge(logits_done, c + 1)
                act.copy(logits[:, c * HALF:(c + 1) * HALF], psO[0:H, (c % 2) * HALF:(c % 2 + 1) * HALF]).then_inc(logits_kept, 1)
            act.wait_ge(logits_turned, 1)
            act.activation(g_exp[:, :, :], psO[:, 0:G * H], ACT.Exp, scale=-1.0).then_inc(gate_exp, 1)
            for g in range(G):
                act.wait_ge(v_done, g + 1)
                r = g // 2
                if g % 2 == 0 and r >= STAGES:
                    act.wait_ge(v_stored[r % STAGES], 16 * (r // STAGES))
                act.copy(v_stage[:, r % STAGES, :, g % 2, :], bank(g % 4).rearrange("p (h d) -> p h d", d=DH)).then_inc(v_kept, 1)
                if g == GATES_AT:
                    act.wait_ge(gate_turned, 1)
                    act.copy(g_unitT[:, :], psO[:, HALF:HALF + P]).then_inc(gate_row, 1)

            def keep_num(w):
                act.wait_ge(pv_done, NT * (w + 1))
                if not (isinstance(w, int) and w == 0):
                    act.wait_ge(out_split, 3 * w)
                    act.wait_ge(den_moved, 16 * w)
                    act.wait_ge(o_set, 32 * w)
                act.copy(num[:, :], psO[0:DH + 1, :]).then_inc(num_kept, 1)

            def head(h, first=False, last=False):
                for b in range(B):
                    u = unit(h, b)
                    if not last:
                        keep_qk_hi(u + 2, b)
                    if not (first and b == 0):
                        keep_num(u - 1)
                    for t in range(NT):
                        act.wait_ge(scores_done, NT * u + t + 1)
                        if not (first and b == 0 and t < 2):
                            act.wait_ge(lo_done, NT * u + t - 1)
                        act.activation(prob[:, t % 2, :], psS[:, t % 2, :], ACT.Exp, scale=SCALE).then_inc(exp_done, 1)
                        act.wait_ge(exp_done, NT * u + t + 1)
                        if not (first and b == 0 and t < NPH):
                            act.wait_ge(pv_done, NT * u + t - NPH + 1)
                        act.copy(prob_hi[:, t % NPH, :], prob[:, t % 2, :]).then_inc(hi_done, 1)

            head(0, first=True)
            with act.Fori(1, H - 2) as h:
                head(h)
            head(H - 2)
            head(H - 1, last=True)
            keep_num(U - 1)
            act.wait_ge(wo_landed, 32)
            act.copy(wo_hi[:, :, :], wo_raw[:, :, :]).then_inc(wo_split, 1)

        @block.vector
        def _(dve):
            def norm_stats(n):
                for g in range(n % B * NT, (n % B + 1) * NT):
                    if n < B and g % 4 == 0:
                        dve.wait_ge(x_in[g // 4], 16)
                    if n >= B:
                        dve.wait_ge(x1_done, G * (n % B) // B + g % NT + 1)
                    dve.bn_stats(stats[:, g, :], x_sb[:, g, :]).then_inc(stats_done, 1)
                for g in range(n % B * NT, (n % B + 1) * NT):
                    dve.wait_ge(stats_done, NT * n + g % NT + 1)
                    dve.bn_aggr(mean_var[:, g, :], stats[:, g, :]).then_inc(var_done, 1)
                half = slice(n % B * NT, (n % B + 1) * NT)
                dve.wait_ge(var_done, NT * (n + 1))
                dve.tensor_scalar(rstd[:, half], mean_var[:, half, 1], LN_EPS, None, ALU.add).then_inc(eps_added, 1)

            def norm_half(n):
                half = slice(n % B * NT, (n % B + 1) * NT)
                dve.wait_ge(std_done, n + 1)
                dve.reciprocal(rstd[:, half], rstd[:, half]).then_inc(rstd_done, 1)
                dve.wait_ge(rstd_done, n + 1)
                if n >= B:
                    dve.scalar_tensor_tensor(out=shift[:, half], in0=mean_var[:, half, 0], scalar=-1.0, in1=rstd[:, half],
                                             op0=ALU.mult, op1=ALU.mult).then_inc(shift_done, 1)
                    return
                for g in range(n % B * NT, (n % B + 1) * NT):
                    dve.tensor_scalar(xn[:, g, :], x_sb[:, g, :], mean_var[:, g, 0:1], rstd[:, g:g + 1],
                                      ALU.subtract, ALU.mult).then_inc(xn_done, 1)

            dve.memset(v1[:, :, :, :], 0.0).then_inc(v1_cleared, 1)
            norm_stats(0)
            norm_stats(1)
            norm_half(0)
            norm_half(1)
            dve.memset(k1[0][DH:P, :].bitcast(F32), 1.0)
            dve.memset(qm[0][DH:P, :].bitcast(F32), 0.0).then_inc(stacks_cleared[0], 1)
            def weights1(b):
                half = slice(b * NT, (b + 1) * NT)
                dve.wait_ge(exp1_done, b + 1)
                dve.reduce_sum(sum1[:, half], prob1[:, b, :].rearrange("p (t k) -> p t k", k=KEYS), AX.X).then_inc(sum1_done, 1)
                dve.wait_ge(sum1_done, b + 1)
                dve.reciprocal(rsum1[:, half], sum1[:, half]).then_inc(rsum1_done, 1)

            def add_cross(b):
                dve.wait_ge(rsum1_done, b + 1)
                for g in range(b * NT, (b + 1) * NT):
                    dve.wait_ge(out1_done, g // 2 + 1)
                    dve.scalar_tensor_tensor(out=x_sb[:, g, :], in0=pair_bank(g), scalar=rsum1[:, g:g + 1],
                                             in1=x_sb[:, g, :], op0=ALU.mult, op1=ALU.add).then_inc(x1_done, 1)

            def keep_xT_lo(k):
                dve.wait_ge(xT_hi_kept, k + 1)
                view = slice(2 * k * P, (2 * k + 2) * P)
                dve.tensor_tensor(xT_lo[:, :, view].rearrange("p c (g q) -> p g c q", q=P),
                                  bank(k % 4).rearrange("p (g c q) -> p g c q", g=2, c=CC),
                                  xT_hi[:, :, view].rearrange("p c (g q) -> p g c q", q=P),
                                  ALU.subtract).then_inc(xT_lo_kept, 1)

            for b in range(B):
                half = slice(b * NT, (b + 1) * NT)
                dve.wait_ge(sc1_done, b + 1)
                scores1 = psM[:, b * HALF:(b + 1) * HALF].rearrange("p (t k) -> p t k", k=KEYS)
                dve.reduce_max(mx1[:, half], scores1, AX.X).then_inc(max1_done, 1)
                dve.wait_ge(max1_done, b + 1)
                dve.tensor_tensor(prob1[:, b, :].rearrange("p (t k) -> p t k", k=KEYS), scores1,
                                  mx1[:, half].unsqueeze(2).broadcast_to([P, NT, KEYS]), ALU.subtract).then_inc(sub1_done, 1)
                weights1(b)
            add_cross(0)
            norm_stats(2)
            add_cross(1)
            norm_half(2)
            norm_stats(3)
            norm_half(3)
            for k in range(G // 4):
                keep_xT_lo(k)

            def keep_qk_lo(z, b):
                dve.wait_ge(qk_hi_kept, z + 1)
                dve.tensor_tensor(qk_lo[b][:, :], psM[:, :], qk_hi[b][:, :], ALU.subtract).then_inc(qk_lo_kept, 1)

            keep_qk_lo(0, 0)
            for k in range(G // 4, G // 2):
                keep_xT_lo(k)
            keep_qk_lo(1, 1)

            def find_max(v, b, t):
                dve.wait_ge(max_scores, NT * v + t + 1)
                dve.reduce_max(row_max[:, b, t:t + 1], psM[:, :], AX.X).then_inc(max_found, 1)

            def split_max(v):
                dve.wait_ge(max_turned, v + 1)
                if not (isinstance(v, int) and v == 0):
                    dve.wait_ge(max_set, 32 * v)
                dve.tensor_scalar(neg_max[:, 0, :], psS[0:NT, 0, 0:P], -1.0, None, ALU.mult).then_inc(max_split, 1)
                dve.wait_ge(max_split, 2 * v + 1)
                dve.scalar_tensor_tensor(out=neg_max[:, 1, :], in0=psS[0:NT, 0, 0:P], scalar=-1.0, in1=neg_max[:, 0, :],
                                         op0=ALU.mult, op1=ALU.subtract).then_inc(max_split, 1)

            dve.wait_ge(gate_exp, 1)
            dve.tensor_scalar(g_exp[:, :, :], g_exp[:, :, :], 1.0, None, ALU.add).then_inc(gate_step, 1)
            dve.wait_ge(gate_step, 1)
            dve.reciprocal(g_sig[:, :, :], g_exp[:, :, :]).then_inc(gate_step, 1)
            dve.wait_ge(gate_step, 2)
            ahead = xn[:, 0:4, :].rearrange("p g c -> p (g c)").rearrange("p (g h k) -> p g h k", h=H, k=H)
            tied = xn[:, 4:8, :].rearrange("p g c -> p (g c)").rearrange("p (g h k) -> p g h k", h=H, k=H)
            other = g_sig[:, :, :].unsqueeze(2).broadcast_to([P, G, H, H])
            own = g_sig[:, :, :].unsqueeze(3).broadcast_to([P, G, H, H])
            dve.wait_ge(xn_turned, G)
            dve.tensor_tensor(ahead, other, own, ALU.is_gt).then_inc(gate_step, 1)
            dve.tensor_tensor(tied, other, own, ALU.is_equal).then_inc(gate_step, 1)
            dve.wait_ge(gate_step, 4)
            dve.wait_ge(consts_done, 4)
            dve.tensor_tensor(tied, tied, before[:, :, :].unsqueeze(1).broadcast_to([P, G, H, H]), ALU.mult).then_inc(gate_step, 1)
            dve.wait_ge(gate_step, 5)
            dve.tensor_tensor(ahead, ahead, tied, ALU.add).then_inc(gate_step, 1)
            dve.wait_ge(gate_step, 6)
            dve.reduce_sum(g_rank[:, :, :], ahead, AX.X).then_inc(gate_step, 1)
            dve.wait_ge(gate_step, 7)
            dve.tensor_scalar(g_rank[:, :, :], g_rank[:, :, :], float(TOP_K), None, ALU.is_lt).then_inc(gate_step, 1)
            dve.wait_ge(gate_step, 8)
            dve.tensor_tensor(g_unit[:, :].rearrange("p (h b t) -> p b t h", b=B, t=NT),
                              g_rank[:, :, :].rearrange("p (b t) h -> p b t h", b=B),
                              g_sig[:, :, :].rearrange("p (b t) h -> p b t h", b=B), ALU.mult).then_inc(gate_step, 1)
            for t in range(NT):
                find_max(0, 0, t)
                if t == GATES_BACK_AT:
                    dve.wait_ge(gates_back, 16)
                    dve.wait_ge(bo_split, 3)
                    dve.tensor_copy(gate_st[0:H, :], logits[:, :]).then_inc(gate_split, 1)
                    dve.wait_ge(gate_split, 1)
                    dve.tensor_tensor(gate_st[32:32 + H, :], logits[:, :], gate_st[0:H, :], ALU.subtract).then_inc(gate_split, 1)
            split_max(0)
            for r in range(G // 2):
                dve.wait_ge(bias_done, r + 1)
                two = x_sb[:, 2 * r:2 * r + 2, :]
                dve.tensor_tensor(two, psO[:, (r % 2) * HALF:(r % 2 + 1) * HALF].rearrange("p (g c) -> p g c", c=C),
                                  two, ALU.add).then_inc(base_done, 1)

            def low_part(n, t):
                dve.wait_ge(hi_done, n + 1)
                if not (isinstance(n, int) and n < 2):
                    dve.wait_ge(pv_done, n - 1)
                dve.tensor_tensor(prob_lo[:, t % 2, :], prob[:, t % 2, :], prob_hi[:, t % NPH, :], ALU.subtract).then_inc(lo_done, 1)

            def weigh(w):
                dve.wait_ge(den_moved, 16 * (w + 1))
                dve.reciprocal(rden[:, :], den[:, :]).then_inc(rden_done, 1)
                dve.wait_ge(rden_done, w + 1)
                dve.wait_ge(gate_fetched, 16 * (w + 1))
                if not (isinstance(w, int) and w == 0):
                    dve.wait_ge(weight_stored, 16 * w)
                dve.tensor_tensor(weight[:, :], rden[:, :], gate[:, :], ALU.mult).then_inc(weight_done, 1)

            def head(h, first=False, last=False):
                for b in range(B):
                    u = unit(h, b)
                    more = not (last and b == B - 1)
                    if not (first and b == 0):
                        split_max(u)
                        low_part(NT * u - 1, NT - 1)
                    if not last:
                        keep_qk_lo(u + 2, b)
                    for t in range(NT):
                        if more:
                            find_max(u + 1, (b + 1) % B, t)
                        if t < NT - 1:
                            low_part(NT * u + t, t)
                        if t == WEIGH_AT and not (first and b == 0):
                            weigh(u - 1)

            head(0, first=True)
            with dve.Fori(1, H - 2) as h:
                head(h)
            head(H - 2)
            head(H - 1, last=True)
            low_part(NT * U - 1, NT - 1)
            dve.wait_ge(wo_split, 1)
            dve.tensor_tensor(wo_lo[:, :, :], wo_raw[:, :, :], wo_hi[:, :, :], ALU.subtract).then_inc(wo_split, 1)
            weigh(U - 1)

            def finish_tile(g):
                dve.wait_ge(proj_done, g + 1)
                base = (base0, base1)[g // NT]
                src = final_half(g)
                dve.tensor_tensor(base[:, g % NT, :], src, base[:, g % NT, :], ALU.add).then_inc(final_done, 1)

            dve.wait_ge(base_fetched, 32)
            for g in range(NT // 2):
                finish_tile(g)
            dve.wait_ge(wide_fetched, 16 * U)
            dve.tensor_tensor(o_hi[:, :], num[0:DH, :], wide[:, :], ALU.mult).then_inc(out_split, 1)
            dve.tensor_tensor(num[0:DH, :], num[0:DH, :], wide[:, :], ALU.mult).then_inc(out_split, 1)
            dve.wait_ge(out_split, 3 * U - 1)
            dve.tensor_tensor(num[0:DH, :], num[0:DH, :], o_hi[:, :], ALU.subtract).then_inc(out_split, 1)
            for g in range(NT // 2, G):
                finish_tile(g)

        @block.tensor
        def _(pe):
            pe.wait_ge(consts_done, 4)
            pe.wait_ge(ctx_landed, 16 * 7)
            for cc in range(CC):
                pe.transpose(psO[:, cc * P:(cc + 1) * P], ctx_sb[:, cc * P:(cc + 1) * P], ident[:, :])
            for ps, w_sb in ((psO[:, HALF:2 * HALF], wk_sb), (psM[:, 0:HALF], wv_sb)):
                for cc in range(CC):
                    for dd in range(CC):
                        mm = pe.transpose(ps[:, cc * C + dd * P:cc * C + (dd + 1) * P],
                                          w_sb[:, dd, cc * P:(cc + 1) * P], ident[:, :])
            mm.then_inc(ctx_turned, 1)
            def turn_xn(n, k):
                pe.wait_ge((xn_done, xn2_done)[n], 2 * k + 2)
                if n == 0 and k >= 4:
                    pe.wait_ge(xnT_kept, k - 3)
                if n == 1 and k >= 4:
                    pe.wait_ge(xT_lo_kept, k - 3)
                dst = bank(k % 4)
                for j in range(2):
                    for cc in range(CC):
                        mm = pe.transpose(dst[:, (j * CC + cc) * P:(j * CC + cc + 1) * P],
                                          xn[:, 2 * k + j, cc * P:(cc + 1) * P], ident[:, :])
                mm.then_inc(xn_turned, 1)

            pe.wait_ge(ctx_kept, 3)
            for dd in range(CC):
                for cc in range(CC):
                    pe.matmul(psO[:, dd * P:(dd + 1) * P], wkT[:, cc, dd * P:(dd + 1) * P], ctxT[:, cc, :],
                              start=(cc == 0), stop=False)
                pe.matmul(psO[:, dd * P:(dd + 1) * P], bk_sb[:, dd * P:(dd + 1) * P], ones_row[:, :],
                          start=False, stop=True)
                pe.matmul(psM[:, HALF + dd:HALF + dd + 1], bq_sb[:, dd * P:(dd + 1) * P], ones_row[:, 0:1],
                          start=True, stop=True)
            for cc in range(CC):
                pe.matmul(psO[:, HALF:HALF + C], ctxT[:, cc, :], wvT[:, cc, :], start=(cc == 0), stop=False)
            pe.matmul(psO[:, HALF:HALF + C], ones_row[:, :], bv_sb[:, :], start=False, stop=True).then_inc(kv1_done, 1)
            for k in range(2):
                turn_xn(0, k)
            pe.wait_ge(kv1_kept, 2)
            for cc in range(CC):
                for dd in range(CC):
                    pe.matmul(psM[:, cc * P:(cc + 1) * P], wq_sb[:, dd, cc * P:(cc + 1) * P], kT1[:, dd, :],
                              start=(dd == 0), stop=(dd == CC - 1))
            for dd in range(CC):
                mm = pe.matmul(psM[0:1, HALF:HALF + P], bq_col[:, dd:dd + 1], kT1[:, dd, :],
                               start=(dd == 0), stop=(dd == CC - 1))
            mm.then_inc(fold_done, 1)

            for k in range(2, G // 2):
                turn_xn(0, k)
            def turn_prob(b):
                pe.wait_ge(exp1_done, b + 1)
                for pair in range(NT // 2):
                    mm = pe.transpose(bank(b)[:, pair * P:(pair + 1) * P], prob1[:, b, pair * P:(pair + 1) * P], ident[:, :])
                mm.then_inc(prob1_turned, 1)

            pe.wait_ge(fold_kept, 2)
            for b in range(B):
                pe.wait_ge(xnT_kept, G // 4 * (b + 1))
                keys = slice(b * KEYS, (b + 1) * KEYS)
                pe.matmul(psM[:, b * HALF:(b + 1) * HALF], ones_row[:, :],
                          fold_b[:, keys].unsqueeze(1).broadcast_to([1, NT, KEYS]), start=True, stop=False)
                for t in range(NT):
                    if b == 1 and t == NT // 2:
                        turn_prob(0)
                    g = b * NT + t
                    for cc in range(CC):
                        mm = pe.matmul(psM[:, b * HALF + t * KEYS:b * HALF + (t + 1) * KEYS],
                                       xnT[:, cc, g * P:(g + 1) * P], foldT[:, cc, keys],
                                       start=False, stop=(t == NT - 1 and cc == CC - 1))
                mm.then_inc(sc1_done, 1)
            pe.wait_ge(v1_spread, 2 * B)

            def out1(b):
                for g in range(b * NT, (b + 1) * NT, 2):
                    if g >= 8:
                        pe.wait_ge(x1_done, g - 6)
                    t = g % NT
                    for odd in range(2):
                        mm = pe.matmul(pair_bank(g + odd), probT[:, b, t // 2 * P:(t // 2 + 1) * P], v1[:, b, odd, :],
                                       start=True, stop=True)
                    mm.then_inc(out1_done, 1)

            pe.wait_ge(probT_kept, 1)
            out1(0)
            turn_prob(1)
            pe.wait_ge(probT_kept, 2)
            out1(1)
            for k in range(G // 4):
                turn_xn(1, k)

            def project(z, b):
                for n, (w, xT) in enumerate(((wqk_hi, xT_hi), (wqk_hi, xT_lo), (wqk_lo, xT_hi))):
                    for cc in range(CC):
                        for half in range(NH):
                            mm = pe.matmul(psM[:, half * HALF:(half + 1) * HALF], w[:, cc, :],
                                           xT[:, cc, b * T + half * HALF:b * T + (half + 1) * HALF],
                                           start=(n == 0 and cc == 0), stop=(n == 2 and cc == CC - 1))
                mm.then_inc(qk_done, 1)

            def max_tile(v, b, t):
                for half in range(NH):
                    mm = pe.matmul(psM[:, half * HALF:(half + 1) * HALF], qq[b][:, t * P:(t + 1) * P],
                                   kk[b][:, half * HALF:(half + 1) * HALF], start=True, stop=True)
                mm.then_inc(max_scores, 1)

            def turn_max(v, b):
                pe.wait_ge(max_found, NT * (v + 1))
                if not (isinstance(v, int) and v == 0):
                    pe.wait_ge(exp_done, NT * v - 1)
                pe.transpose(psS[0:NT, 0, 0:P], row_max[:, b, :], ident[:, :]).then_inc(max_turned, 1)

            pe.wait_ge(xT_lo_kept, G // 4)
            pe.wait_ge(wqk_split, 2)
            project(0, 0)
            for k in range(G // 4, G // 2):
                turn_xn(1, k)
            pe.wait_ge(xT_lo_kept, G // 2)
            pe.wait_ge(qk_lo_kept, 1)
            project(1, 1)
            pe.wait_ge(ws_split, 2)
            for c in range(4):
                if c >= 2:
                    pe.wait_ge(logits_kept, c - 1)
                for n, (w, xT) in enumerate(((ws_hi, xT_hi), (ws_hi, xT_lo), (ws_lo, xT_hi))):
                    for cc in range(CC):
                        mm = pe.matmul(psO[0:H, (c % 2) * HALF:(c % 2 + 1) * HALF], w[:, cc, :], xT[:, cc, c * HALF:(c + 1) * HALF],
                                       start=(n == 0 and cc == 0), stop=(n == 2 and cc == CC - 1))
                mm.then_inc(logits_done, 1)
            pe.wait_ge(wv_split, 2)
            for g in range(G):
                if g >= 4:
                    pe.wait_ge(v_kept, g - 3)
                terms = ((xT_hi, wv_hi), (xT_hi, wv_lo), (xT_lo, wv_hi))
                for n, (xT, w) in enumerate(terms):
                    for cc in range(CC):
                        mm = pe.matmul(bank(g % 4), xT[:, cc, g * P:(g + 1) * P], w[:, cc, :],
                                       start=(n == 0 and cc == 0), stop=(n == 2 and cc == CC - 1))
                mm.then_inc(v_done, 1)
                if g == 0:
                    pe.wait_ge(logits_kept, 4)
                    for j in range(G):
                        mm = pe.transpose(psO[:, j * H:(j + 1) * H], logits[:, j * P:(j + 1) * P], ident[0:H, 0:H])
                    mm.then_inc(logits_turned, 1)
                t = g - FIRST_MAX
                if t == 0:
                    pe.wait_ge(qk_lo_kept, 2)
                    pe.wait_ge(pairs_set, 64)
                if 0 <= t < NT:
                    if t:
                        pe.wait_ge(max_found, t)
                    max_tile(0, 0, t)
                if g == G - 1:
                    pe.wait_ge(v_kept, G - 3)
                    turn_max(0, 0)
                if g == GATES_AT:
                    pe.wait_ge(gate_step, 9)
                    pe.transpose(psO[:, HALF:HALF + P], g_unit[:, :], ident[:, :]).then_inc(gate_turned, 1)
            pe.wait_ge(v_kept, G)
            pe.wait_ge(gate_split, 2)
            pe.wait_ge(gate_row, 1)
            for r in range(G // 2):
                if r >= 2:
                    pe.wait_ge(base_done, r - 1)
                for g in (2 * r, 2 * r + 1):
                    dst = psO[:, (r % 2) * HALF + g % 2 * C:(r % 2) * HALF + (g % 2 + 1) * C]
                    for w in (bo_hi, bo_lo):
                        mm = pe.matmul(dst, gate_st[:, g * P:(g + 1) * P], w[:, :], start=(w is bo_hi), stop=(w is bo_lo))
                mm.then_inc(bias_done, 1)

            def score_tile(u, b, t, first):
                if not (first and t < 2):
                    pe.wait_ge(exp_done, NT * u + t - 1)
                for half in range(NH):
                    pe.matmul(psS[:, t % 2, half * HALF:(half + 1) * HALF], kk[b][:, t * P:(t + 1) * P],
                              qq[b][:, half * HALF:(half + 1) * HALF], start=True, stop=False)
                if t == 0:
                    pe.wait_ge(max_set, 32 * (u + 1))
                for half in range(NH):
                    mm = pe.matmul(psS[:, t % 2, half * HALF:(half + 1) * HALF], k1[b][:, t * P:(t + 1) * P],
                                   qm[b][:, half * HALF:(half + 1) * HALF], start=False, stop=True)
                mm.then_inc(scores_done, 1)

            def pv_tile(w, b, t, between=None):
                if t == 0:
                    pe.wait_ge(v_split, 2 * (w + 1))
                    if isinstance(w, int) and w == 0:
                        pe.wait_ge(base_done, NT)
                    else:
                        pe.wait_ge(num_kept, w)
                pe.wait_ge(lo_done, NT * w + t + 1)
                hi, lo = prob_hi[:, t % NPH, :], prob_lo[:, t % 2, :]
                with_ones, v_lo = v_st[b][:, t, 0:DH + 2], v_st[b][:, t, VLO:VLO + DH]
                for half in range(NH):
                    mm = pe.matmul(psO[0:DH + 2, half * HALF:(half + 1) * HALF], with_ones,
                                   hi[:, half * HALF:(half + 1) * HALF], start=(t == 0), stop=False)
                    if t == NT - 1 - LAG and half == 0:
                        mm.then_inc(stacks_free, 1)
                for half in range(NH):
                    pe.matmul(psO[0:DH, half * HALF:(half + 1) * HALF], v_lo,
                              hi[:, half * HALF:(half + 1) * HALF], start=False, stop=False)
                if between:
                    between()
                for half in range(NH):
                    mm = pe.matmul(psO[0:DH + 2, half * HALF:(half + 1) * HALF], with_ones,
                                   lo[:, half * HALF:(half + 1) * HALF], start=False, stop=(t == NT - 1))
                mm.then_inc(pv_done, 1)

            def head(h, first=False, last=False):
                for b in range(B):
                    u = unit(h, b)
                    more = not (last and b == B - 1)

                    def next_max(m):
                        if not more:
                            return
                        if m == 0:
                            pe.wait_ge(pairs_set, 64 * (u + 2))
                            if last:
                                pe.wait_ge(qk_lo_kept, U)
                            else:
                                pe.wait_ge(qk_lo_kept, u + 3)
                        else:
                            pe.wait_ge(max_found, NT * (u + 1) + m)
                        max_tile(u + 1, (b + 1) % B, m)

                    before_it = not (first and b == 0)
                    if before_it:
                        pv_tile(u - 1, (b + 1) % B, NT - LAG, lambda: turn_max(u, b))
                    pe.wait_ge(rest_set[b], 32 * (h + 1))
                    if not last:
                        if b == 0:
                            pe.wait_ge(wqk_split, 2 * (h + 2))
                        project(u + 2, b)
                    if before_it:
                        pv_tile(u - 1, (b + 1) % B, NT - 1)
                    pe.wait_ge(max_split, 2 * (u + 1))
                    for t in range(NT):
                        score_tile(u, b, t, first and b == 0)
                        if t < LAG:
                            next_max(t)
                        else:
                            pv_tile(u, b, t - LAG, lambda: next_max(t))

            head(0, first=True)
            with pe.Fori(1, H - 2) as h:
                head(h)
            head(H - 2)
            head(H - 1, last=True)
            for t in range(NT - LAG, NT):
                pv_tile(U - 1, B - 1, t)
            def project_out(g, heads):
                b, t = divmod(g, NT)
                for h in heads:
                    for w in (wo_hi, wo_lo):
                        mm = pe.matmul(final_half(g), o_st[:, b, h, t * P:(t + 1) * P], w[:, h, :],
                                       start=(h == 0 and w is wo_hi), stop=(h == H - 1 and w is wo_lo))
                return mm

            pe.wait_ge(wo_split, 2)
            pe.wait_ge(o_set, 32 * (U - 1))
            for g in range(NT):
                if g >= 2:
                    pe.wait_ge(final_done, g - 1)
                project_out(g, range(H)).then_inc(proj_done, 1)
            pe.wait_ge(num_kept, U)
            pe.wait_ge(final_done, NT)
            for g in range(NT, G):
                project_out(g, range(H - 1))
            pe.wait_ge(last_o_set, 32)
            for g in range(NT, G):
                project_out(g, range(H - 1, H)).then_inc(proj_done, 1)


_INS = ['x', 'ctx_1024', 'L0_xattn_Wq', 'L0_xattn_bq', 'L0_xattn_Wk', 'L0_xattn_bk', 'L0_xattn_Wv',
        'L0_xattn_bv', 'L0_ffn_Wq', 'L0_ffn_Wkv', 'L0_ffn_Ws', 'L0_ffn_Wo', 'L0_ffn_bo']


def kernel(**inputs):
    import numpy as _np
    import concourse.bacc as _bacc
    from concourse import mybir as _mybir
    from concourse.bass_utils import run_bass_kernel_spmd as _run

    nc = _bacc.Bacc("TRN2", target_bir_lowering=False, num_devices=1)
    arrays, args = {}, []
    for name in _INS:
        a = _np.ascontiguousarray(inputs[name])
        arrays[f"in_{name}_dram"] = a
        args.append(nc.dram_tensor(f"in_{name}_dram", a.shape, _mybir.dt.from_np(a.dtype), kind="ExternalInput").ap())
    shape = inputs['x'].shape
    args.append(nc.dram_tensor("out_0_dram", shape, _mybir.dt.from_np(_np.dtype("float32")), kind="ExternalOutput").ap())
    build(nc, *args)
    r = _run(nc, [arrays], core_ids=[0])
    return r.results[0]["out_0_dram"]
```

```python
from contextlib import ExitStack

import concourse.bass as bass
from concourse import mybir

P = 128
F32 = mybir.dt.float32
F32R = mybir.dt.float32r
ALU = mybir.AluOpType
ACT = mybir.ActivationFunctionType
AX = mybir.AxisListType

LN_EPS = 1e-5
TOP_K = 3


def build(nc, x, ctx_in, wq1, bq1, wk1, bk1, wv1, bv1, wq2, wkv2, ws2, wo2, bo2, out):
    B, T, C = x.shape
    KEYS = ctx_in.shape[1]
    H, DH, _ = wo2.shape
    HD = H * DH
    CC = C // P
    NT = T // P
    G = B * NT
    U = B * H
    SCALE = float(DH) ** -0.5
    HALF = 512
    NH = T // HALF
    ONES = DH
    VLO = DH + 2
    VW = 2 * DH + 2
    NPH = 4
    LAG = 2
    FIRST_MAX, GATES_AT = 6, 7
    ACT_NORMS = 10
    BIAS_AT = 12
    POOL_TILE = 4
    WEIGH_AT = 2
    WL = 16
    WR = T // WL
    assert B == 2 and C == CC * P and B * KEYS == P and 2 * DH == P and U * NT == P and NT == 8

    base_d = nc.dram_tensor("base_d", (P, G, C), F32, kind="Internal").ap()
    v_d = nc.dram_tensor("v_d", (B, H, P, NT * DH), F32, kind="Internal").ap()
    gate_d = nc.dram_tensor("gate_d", (3, P, P), F32, kind="Internal").ap()
    weight_d = nc.dram_tensor("weight_d", (B, T), F32, kind="Internal").ap()

    with ExitStack() as top:
        def sem(name):
            return top.enter_context(nc.semaphore(name))

        def sb(name, shape, dt=F32, stack=top):
            return stack.enter_context(nc.sbuf_tensor(name, shape, dt))

        ident = sb("ident", [P, P])
        ones_row = sb("ones_row", [1, P])
        zero = sb("zero", [P, 1])
        wqk_raw = sb("wqk_raw", [P, CC, P])
        wqk_hi = sb("wqk_hi", [P, CC, P], F32R)
        wqk_lo = sb("wqk_lo", [P, CC, P], F32R)
        ws_raw = sb("ws_raw", [P, CC, H])
        ws_parts = sb("ws_parts", [P, CC, 2, H], F32R)
        qk_hi = [sb(f"qk_hi{b}", [P, T], F32R) for b in range(B)]
        qk_lo = [sb(f"qk_lo{b}", [P, T], F32R) for b in range(B)]
        stacks0 = [sb(f"{n}0", [P, T], F32R) for n in ("kk", "qq", "k1", "qm")]
        v_raw = sb("v_raw", [P, NT, DH])
        v_st = [sb(f"v_st{b}", [P, NT, VW], F32R) for b in range(B)]
        row_max = sb("row_max", [P, B, NT])
        max_parts = sb("max_parts", [P, 2, NT], F32R)
        neg_max = sb("neg_max", [2 * NT, P], F32R)
        den = sb("den", [WR, WL])
        rden = sb("rden", [WR, WL])
        gate = sb("gate", [WR, WL])
        weight = sb("weight", [WR, WL])

        def overlay(*stages):
            widest, got = 0, []
            for named in stages:
                size = sum(w * 4 for _, w in ((n, _width(s)) for n, s, _ in named))
                widest = max(widest, size)
                with ExitStack() as own:
                    got.append([sb(n, s, d, own) for n, s, d in named])
            sb(f"room{len(rooms)}", [P, widest // 4])
            rooms.append(widest)
            return got

        def _width(shape):
            n = 1
            for s in shape[1:]:
                n *= s
            return n

        rooms = []
        (wv_raw, wv_hi, wv_lo), stacks1 = overlay(
            [("wv_raw", [P, CC, HD], F32), ("wv_hi", [P, CC, HD], F32R), ("wv_lo", [P, CC, HD], F32R)],
            [(f"{n}1", [P, T], F32R) for n in ("kk", "qq", "k1", "qm")])
        kk, qq, k1, qm = zip(stacks0, stacks1)
        (xT_hi, xT_lo), (wo_raw, wo_hi, wo_lo, base0) = overlay(
            [("xT_hi", [P, CC, B * T], F32R), ("xT_lo", [P, CC, B * T], F32R)],
            [("wo_raw", [P, H, C], F32), ("wo_hi", [P, H, C], F32R), ("wo_lo", [P, H, C], F32R),
             ("base0", [P, NT, C], F32)])
        (x_sb, xn, xnT, logits, gate_st), (o_st,) = overlay(
            [("x_sb", [P, G, C], F32), ("xn", [P, G, C], F32), ("xnT", [P, CC, B * T], F32),
             ("logits", [2 * H, B * T], F32), ("gate_st", [P, B * T], F32R)],
            [("o_st", [P, B, H, T], F32R)])
        (ctx_sb, ctxT, wk_sb, wv_sb, wq_sb, wkT, wvT, kT1, foldT, fold_b, v1, prob1, probT,
         bk_sb, bq_sb, bq_col, bv_sb, bo_raw, bo_st, shift,
         stats, mean_var, rstd, mx1, sum1, rsum1, g_exp, g_sig, g_rank, g_unit, g_hi, g_lo, g_unitT, before), \
            (prob, prob_hi, prob_lo, num, wide, o_hi) = overlay(
            [("ctx_sb", [P, C], F32), ("ctxT", [P, CC, P], F32), ("wk_sb", [P, CC, C], F32),
             ("wv_sb", [P, CC, C], F32), ("wq_sb", [P, CC, C], F32), ("wkT", [P, CC, C], F32),
             ("wvT", [P, CC, C], F32), ("kT1", [P, CC, P], F32), ("foldT", [P, CC, P], F32),
             ("fold_b", [1, P], F32), ("v1", [P, B, 2, C], F32), 
             ("prob1", [P, B, NT * KEYS], F32), ("probT", [P, B, NT * KEYS], F32), ("bk_sb", [1, C], F32),
             ("bq_sb", [1, C], F32), ("bq_col", [P, CC], F32), ("bv_sb", [1, C], F32), ("bo_raw", [P, C], F32), ("bo_st", [P, C], F32R),
             ("shift", [P, G], F32),
             ("stats", [P, G, 6], F32), ("mean_var", [P, G, 2], F32), ("rstd", [P, G], F32),
             ("mx1", [P, G], F32), ("sum1", [P, G], F32), ("rsum1", [P, G], F32),
             ("g_exp", [P, G, H], F32), ("g_sig", [P, G, H], F32), ("g_rank", [P, G, H], F32),
             ("g_unit", [P, P], F32), ("g_hi", [P, P], F32R), ("g_lo", [P, P], F32R),
             ("g_unitT", [P, 3, P], F32), ("before", [P, H, H], F32)],
            [("prob", [P, 2, T], F32), ("prob_hi", [P, NPH, T], F32R),
             ("prob_lo", [P, 2, T], F32R), ("num", [DH + 1, T], F32), ("wide", [DH, T], F32),
             ("o_hi", [DH, T], F32R)])
        num_last, wide_last, o_hi_last = prob[0:DH + 1, 0, :], prob[0:DH, 1, :], prob_hi[0:DH, 0, :]
        base1 = wo_raw[:, :, :].rearrange("p h c -> p (h c)")[:, 0:NT * C].rearrange("p (t c) -> p t c", c=C)

        STAGES = 4
        v_stage = xnT[:, :, :].rearrange("p c n -> p (c n)").rearrange("p (s h t d) -> p s h t d", s=STAGES, h=H, t=2)

        psS = top.enter_context(nc.psum_tensor("psS", [P, 2, T], F32))
        psM = top.enter_context(nc.psum_tensor("psM", [P, T], F32))
        psO = top.enter_context(nc.psum_tensor("psO", [P, T], F32))

        def bank(n):
            return psS[:, n // 2, (n % 2) * HALF:(n % 2 + 1) * HALF]

        def turned_bank(k):
            return (bank(0), bank(1), bank(2), bank(3), psO[:, 0:HALF], psO[:, HALF:2 * HALF], bank(0), bank(1))[k]

        def pair_bank(g):
            r = g // 2 % 4
            whole = bank(2 + r) if r < 2 else psO[:, (r - 2) * HALF:(r - 1) * HALF]
            return whole[:, g % 2 * C:(g % 2 + 1) * C]

        def final_half(g):
            sums = (psM[:, 0:HALF], psM[:, HALF:2 * HALF])
            if g < NT:
                return (sums + (bank(0), bank(1), bank(2), bank(3), bank(0), bank(1)))[g][:, 0:C]
            return (sums + (psO[:, 0:HALF], psO[:, HALF:2 * HALF], bank(0), bank(1), bank(2), bank(3)))[g - NT][:, 0:C]

        x_in = [sem(f"x_in{i}") for i in range(4)]
        ctx_landed = sem("ctx_landed")
        wqk_landed = sem("wqk_landed")
        wv_landed = sem("wv_landed")
        small_landed = sem("small_landed")
        consts_set = sem("consts_set")
        consts_done = sem("consts_done")
        stats_done = sem("stats_done")
        var_done = sem("var_done")
        eps_added = sem("eps_added")
        std_done = sem("std_done")
        rstd_done = sem("rstd_done")
        xn_done = sem("xn_done")
        shift_done = sem("shift_done")
        xn2_done = sem("xn2_done")
        ctx_turned = sem("ctx_turned")
        ctx_kept = sem("ctx_kept")
        kv1_done = sem("kv1_done")
        kv1_kept = sem("kv1_kept")
        fold_done = sem("fold_done")
        fold_kept = sem("fold_kept")
        xn_turned = sem("xn_turned")
        xnT_kept = sem("xnT_kept")
        xT_hi_kept = sem("xT_hi_kept")
        xT_lo_kept = sem("xT_lo_kept")
        sc1_done = sem("sc1_done")
        max1_done = sem("max1_done")
        sub1_done = sem("sub1_done")
        exp1_done = sem("exp1_done")
        sum1_done = sem("sum1_done")
        rsum1_done = sem("rsum1_done")
        prob1_turned = sem("prob1_turned")
        probT_kept = sem("probT_kept")
        out1_done = sem("out1_done")
        x1_done = sem("x1_done")
        cross_kept = sem("cross_kept")
        x1b_done = sem("x1b_done")
        wv_split = sem("wv_split")
        v_done = sem("v_done")
        v_kept = sem("v_kept")
        v_stored = [sem(f"v_stored{i}") for i in range(STAGES)]
        ws_split = sem("ws_split")
        logits_done = sem("logits_done")
        logits_kept = sem("logits_kept")
        v1_spread = sem("v1_spread")
        bo_cleared = sem("bo_cleared")
        v1_cleared = sem("v1_cleared")
        gate_row = sem("gate_row")
        logits_summed = sem("logits_summed")
        gates_back = sem("gates_back")
        bo_split = sem("bo_split")
        logits_turned = sem("logits_turned")
        gate_exp = sem("gate_exp")
        gate_step = sem("gate_step")
        gate_turned = sem("gate_turned")
        gate_stored = sem("gate_stored")
        bias_done = sem("bias_done")
        base_done = sem("base_done")
        base_stored = sem("base_stored")

        wqk_split = sem("wqk_split")
        qk_done = sem("qk_done")
        qk_hi_kept = sem("qk_hi_kept")
        qk_lo_kept = sem("qk_lo_kept")
        stacks_cleared = [sem(f"stacks_cleared{b}") for b in range(B)]
        stacks_free = sem("stacks_free")
        pairs_set = sem("pairs_set")
        rest_set = [sem(f"rest_set{b}") for b in range(B)]
        v_fetched = sem("v_fetched")
        v_split = sem("v_split")
        max_scores = sem("max_scores")
        max_found = sem("max_found")
        max_turned = sem("max_turned")
        max_kept = sem("max_kept")
        max_split = sem("max_split")
        max_set = sem("max_set")
        scores_done = sem("scores_done")
        exp_done = sem("exp_done")
        hi_done = sem("hi_done")
        lo_done = sem("lo_done")
        pool_lo_done = sem("pool_lo_done")
        pv_done = sem("pv_done")
        num_kept = sem("num_kept")
        den_moved = sem("den_moved")
        gate_fetched = sem("gate_fetched")
        rden_done = sem("rden_done")
        weight_done = sem("weight_done")
        weight_stored = sem("weight_stored")
        wide_fetched = sem("wide_fetched")
        out_split = sem("out_split")
        last_split = sem("last_split")
        o_set = sem("o_set")
        last_o_set = sem("last_o_set")
        wo_landed = sem("wo_landed")
        wo_split = sem("wo_split")
        base_fetched = sem("base_fetched")
        proj_done = sem("proj_done")
        final_done = sem("final_done")
        out_stored = sem("out_stored")

        x_tiles = x.rearrange("b (t p) c -> p (b t) c", p=P)
        out_tiles = out.rearrange("b (t p) c -> p (b t) c", p=P)
        wq_heads = wq2.rearrange("(cc p) n -> p cc n", p=P)
        wkv_heads = wkv2.rearrange("(cc p) n -> p cc n", p=P)

        gate_rows = gate_d[0].rearrange("r (a i) -> (r a) i", i=WL)

        def unit(h, b):
            return B * h + b

        def wait_lo(eng, u, t):
            if t == POOL_TILE:
                eng.wait_ge(pool_lo_done, u + 1)
            else:
                eng.wait_ge(lo_done, (NT - 1) * u + (t + 1 if t < POOL_TILE else t))

        block = top.enter_context(nc.Block())

        @block.sync
        def _(sp):
            for i in range(4):
                w = G // 4
                sp.dma_start(x_sb[:, i * w:(i + 1) * w, :], x_tiles[:, i * w:(i + 1) * w, :]).then_inc(x_in[i], 16)
                if i == 0:
                    sp.dma_start(ctx_sb[:, :], ctx_in.rearrange("b k c -> (b k) c")).then_inc(ctx_landed, 16)
                    for w_sb, w_in in ((wk_sb, wk1), (wv_sb, wv1), (wq_sb, wq1)):
                        sp.dma_start(w_sb[:, :, :], w_in.rearrange("(dd p) c -> p dd c", p=P)).then_inc(ctx_landed, 16)
                    for b_sb, b_in in ((bk_sb, bk1), (bq_sb, bq1), (bv_sb, bv1)):
                        sp.dma_start(b_sb[:, :], b_in.rearrange("(a c) -> a c", a=1)).then_inc(ctx_landed, 16)
            sp.dma_start(ws_raw[:, :, :], ws2.rearrange("(cc p) h -> p cc h", p=P)).then_inc(small_landed, 16)
            sp.wait_ge(bo_cleared, 1)
            for row in (0, 32, 64, 96):
                sp.dma_start(bo_raw[row:row + H, :], bo2).then_inc(small_landed, 16)
            sp.dma_start(wv_raw[:, :, :], wkv_heads[:, :, HD:2 * HD]).then_inc(wv_landed, 16)

            def fetch_wqk(h):
                if not (isinstance(h, int) and h == 0):
                    sp.wait_ge(wqk_split, 2 * h)
                sp.dma_start(wqk_raw[:, :, 0:DH], wq_heads[:, :, bass.ds(h * DH, DH)]).then_inc(wqk_landed, 16)
                sp.dma_start(wqk_raw[:, :, DH:2 * DH], wkv_heads[:, :, bass.ds(h * DH, DH)]).then_inc(wqk_landed, 16)

            def stack_pairs(v, b):
                if isinstance(v, int) and v < B:
                    if v == 1:
                        sp.wait_ge(v_done, G)
                    sp.wait_ge(qk_lo_kept, v + 1)
                else:
                    sp.wait_ge(stacks_free, v - 1)
                hi, lo = qk_hi[b], qk_lo[b]
                for dst, src in ((kk[b][0:DH, :], hi[DH:P, :]), (kk[b][DH:P, :], hi[DH:P, :]),
                                 (qq[b][0:DH, :], hi[0:DH, :]), (qq[b][DH:P, :], lo[0:DH, :])):
                    sp.dma_start(dst.bitcast(F32), src.bitcast(F32)).then_inc(pairs_set, 16)

            def stack_rest(b, first=False):
                if first:
                    sp.wait_ge(stacks_cleared[b], 1)
                for dst, src in ((k1[b][0:DH, :], qk_lo[b][DH:P, :]), (qm[b][0:DH, :], qk_hi[b][0:DH, :])):
                    sp.dma_start(dst.bitcast(F32), src.bitcast(F32)).then_inc(rest_set[b], 16)

            def fetch_v(v, h, b):
                if not (isinstance(v, int) and v == 0):
                    sp.wait_ge(v_split, 2 * v)
                sp.dma_start(v_raw[:, :, :], v_d[b, bass.ds(h, 1)].rearrange("a p (t d) -> p (a t) d", d=DH)).then_inc(v_fetched, 16)

            def set_max(v, b):
                sp.wait_ge(max_kept, v + 1)
                sp.dma_start(qm[b][DH:DH + 2, :].bitcast(F32).rearrange("a (t p) -> a t p", p=P),
                             neg_max[:, :].bitcast(F32)).then_inc(max_set, 16)

            def weigh(w, b, num=num, wide=wide):
                first = isinstance(w, int) and w == 0
                if not first:
                    sp.wait_ge(weight_done, w)
                sp.dma_start(gate[:, :], gate_rows[bass.ds(w * WR, WR), :]).then_inc(gate_fetched, 16)
                sp.wait_ge(num_kept, w + 1)
                sp.dma_start(den[:, :], num[DH:DH + 1, :].rearrange("a (t p) -> a t p", p=WL)).then_inc(den_moved, 16)
                sp.wait_ge(weight_done, w + 1)
                sp.dma_start(weight_d[b].rearrange("(t p) -> t p", p=WL), weight[:, :]).then_inc(weight_stored, 16)
                sp.wait_ge(weight_stored, 16 * (w + 1))
                sp.dma_start(wide[:, :], weight_d[b:b + 1, :].broadcast_to([DH, T])).then_inc(wide_fetched, 16)

            fetch_wqk(0)
            fetch_wqk(1)
            stack_pairs(0, 0)
            stack_rest(0, first=True)
            sp.wait_ge(gate_row, 1)
            sp.dma_start(gate_d.rearrange("k r i -> r k i"), g_unitT[:, :, :]).then_inc(gate_stored, 16)
            sp.wait_ge(gate_stored, 16)
            sp.wait_ge(bo_split, 3)
            for row in (0, 32, 64, 96):
                sp.dma_start(gate_st[row:row + H, :].bitcast(F32),
                             gate_d[1 + row // 32 % 2].rearrange("(h g) i -> h (g i)", h=H)).then_inc(gates_back, 16)
            set_max(0, 0)
            stack_pairs(1, 1)
            for i in range(STAGES):
                sp.wait_ge(v_stored[i], 16 * (G // 2 // STAGES))
            fetch_v(0, 0, 0)
            sp.wait_ge(base_done, NT)
            sp.dma_start(base_d, x_sb[:, :, :]).then_inc(base_stored, 16)

            def head(h, first=False, last=False, ahead=True):
                for b in range(B):
                    u = unit(h, b)
                    if not (last and b == B - 1):
                        stack_rest((b + 1) % B, first and b == 0)
                        fetch_v(u + 1, h + (b + 1) // B, (b + 1) % B)
                    if b == 0 and ahead:
                        fetch_wqk(h + 2)
                    if last and b == 0:
                        sp.wait_ge(qk_done, U)
                        for part in range(2):
                            sp.dma_start(wo_raw[part * DH:(part + 1) * DH, :, :], wo2.rearrange("h d c -> d h c")).then_inc(wo_landed, 16)
                        sp.dma_start(base0[:, :, :], base_d[:, 0:NT, :]).then_inc(base_fetched, 16)
                    if not (first and b == 0):
                        weigh(u - 1, (b + 1) % B)
                    if not last:
                        stack_pairs(u + 2, b)
                    if not (last and b == B - 1):
                        set_max(u + 1, (b + 1) % B)

            head(0, first=True)
            with sp.Fori(1, H - 2) as h:
                head(h)
            head(H - 2, ahead=False)
            head(H - 1, last=True, ahead=False)
            sp.wait_ge(wo_split, 5)
            sp.dma_start(base1, base_d[:, NT:G, :]).then_inc(base_fetched, 16)
            weigh(U - 1, B - 1, num_last, wide_last)
            sp.wait_ge(last_split, 3)
            for part, src in enumerate((o_hi_last, num_last)):
                sp.dma_start(o_st[part * DH:(part + 1) * DH, B - 1, H - 1, :].bitcast(F32), src[0:DH, :].bitcast(F32)).then_inc(last_o_set, 16)
            for g in range(0, G, 2):
                sp.wait_ge(final_done, g + 2)
                t = g % NT
                src = base0[:, t:t + 2, :] if g < NT else base1[:, t:t + 2, :]
                sp.dma_start(out_tiles[:, g:g + 2, :], src).then_inc(out_stored, 16)
            sp.wait_ge(out_stored, 16 * (G // 2))

        @block.gpsimd
        def _(pool):
            nc.gpsimd.memset(ident[:, :], 0.0).then_inc(consts_set, 1)
            nc.gpsimd.memset(ones_row[:, :], 1.0).then_inc(consts_done, 1)
            nc.gpsimd.memset(before[:, :, :], 1.0).then_inc(consts_set, 1)
            nc.gpsimd.memset(zero[:, :], 0.0).then_inc(consts_set, 1)
            pool.wait_ge(consts_set, 3)
            nc.gpsimd.affine_select(out=ident[:, :], in_=ident[:, :], compare_op=ALU.not_equal, fill=1.0,
                                    base=0, pattern=[[-1, P]], channel_multiplier=1).then_inc(consts_done, 1)
            nc.gpsimd.affine_select(out=before[:, :, :], in_=before[:, :, :], compare_op=ALU.is_gt, fill=0.0,
                                    base=0, pattern=[[1, H], [-1, H]], channel_multiplier=0).then_inc(consts_done, 1)
            for b in range(B):
                last = nc.gpsimd.memset(v_st[b][:, :, ONES:ONES + 2].bitcast(F32), 1.0)
            last.then_inc(consts_done, 1)

            def round_to(dst, src):
                return nc.gpsimd.tensor_tensor(dst, src, zero[:, :].unsqueeze(2).broadcast_to(src.shape), ALU.add)

            def split_wqk(h):
                pool.wait_ge(wqk_landed, 32 * (h + 1))
                if not (isinstance(h, int) and h == 0):
                    pool.wait_ge(qk_done, B * h)
                round_to(wqk_hi[:, :, :], wqk_raw[:, :, :]).then_inc(wqk_split, 1)
                pool.wait_ge(wqk_split, 2 * h + 1)
                nc.gpsimd.tensor_tensor(wqk_lo[:, :, :], wqk_raw[:, :, :], wqk_hi[:, :, :], ALU.subtract).then_inc(wqk_split, 1)

            def split_v(v, b):
                pool.wait_ge(v_fetched, 16 * (v + 1))
                if not (isinstance(v, int) and v < B):
                    pool.wait_ge(pv_done, NT * (v - 1))
                round_to(v_st[b][:, :, 0:DH], v_raw[:, :, :]).then_inc(v_split, 1)
                pool.wait_ge(v_split, 2 * v + 1)
                nc.gpsimd.tensor_tensor(v_st[b][:, :, VLO:VLO + DH], v_raw[:, :, :], v_st[b][:, :, 0:DH],
                                        ALU.subtract).then_inc(v_split, 1)

            def finish(w, h, b):
                def store(part, src):
                    pool.dma_start(o_st[part * DH:(part + 1) * DH, b, bass.ds(h, 1), :].bitcast(F32).rearrange("p a t -> p (a t)"),
                                   src[0:DH, :].bitcast(F32)).then_inc(o_set, 16)

                pool.wait_ge(wide_fetched, 16 * (w + 1))
                if not (isinstance(w, int) and w == 0):
                    pool.wait_ge(o_set, 32 * w)
                nc.gpsimd.tensor_tensor(o_hi[:, :], num[0:DH, :], wide[:, :], ALU.mult).then_inc(out_split, 1)
                if isinstance(w, int) and w == 0:
                    pool.wait_ge(base_stored, 16)
                pool.wait_ge(out_split, 3 * w + 1)
                store(0, o_hi)
                nc.gpsimd.tensor_tensor(num[0:DH, :], num[0:DH, :], wide[:, :], ALU.mult).then_inc(out_split, 1)
                pool.wait_ge(out_split, 3 * w + 2)
                nc.gpsimd.tensor_tensor(num[0:DH, :], num[0:DH, :], o_hi[:, :], ALU.subtract).then_inc(out_split, 1)
                pool.wait_ge(out_split, 3 * w + 3)
                store(1, num)

            def low_part(u):
                t = POOL_TILE
                pool.wait_ge(hi_done, NT * u + t + 1)
                pool.wait_ge(pv_done, NT * u + t - 1)
                nc.gpsimd.tensor_tensor(prob_lo[:, t % 2, :], prob[:, t % 2, :], prob_hi[:, t % NPH, :], ALU.subtract).then_inc(pool_lo_done, 1)

            def store_v(r):
                pool.wait_ge(v_kept, 2 * r + 2)
                b, t = divmod(2 * r, NT)
                pool.dma_start(v_d[b, :, :, t * DH:(t + 2) * DH].rearrange("h p n -> p h n"),
                               v_stage[:, r % STAGES].rearrange("p h t d -> p h (t d)")).then_inc(v_stored[r % STAGES], 16)

            nc.gpsimd.memset(bo_raw[:, :], 0.0).then_inc(bo_cleared, 1)
            split_wqk(0)
            pool.wait_ge(small_landed, 16 * 5)
            nc.gpsimd.tensor_tensor(ws_parts[:, :, 0, :], ws_raw[:, :, :], zero[:, :].unsqueeze(2).broadcast_to([P, CC, H]),
                                    ALU.add).then_inc(ws_split, 1)
            pool.wait_ge(ws_split, 1)
            nc.gpsimd.tensor_tensor(ws_parts[:, :, 1, :], ws_raw[:, :, :], ws_parts[:, :, 0, :], ALU.subtract).then_inc(ws_split, 1)
            pool.wait_ge(wv_landed, 16)
            round_to(wv_hi[:, :, :], wv_raw[:, :, :]).then_inc(wv_split, 1)
            pool.wait_ge(wv_split, 1)
            nc.gpsimd.tensor_tensor(wv_lo[:, :, :], wv_raw[:, :, :], wv_hi[:, :, :], ALU.subtract).then_inc(wv_split, 1)
            nc.gpsimd.tensor_copy(bo_st[:, :], bo_raw[:, :]).then_inc(bo_split, 1)
            pool.wait_ge(bo_split, 1)
            nc.gpsimd.tensor_tensor(bo_st[DH:P, :], bo_raw[DH:P, :], bo_st[DH:P, :], ALU.subtract).then_inc(bo_split, 1)
            pool.wait_ge(bo_split, 2)
            nc.gpsimd.memset(gate_st[:, :].bitcast(F32), 0.0).then_inc(bo_split, 1)
            for t in range(NT):
                pool.wait_ge(cross_kept, t + 1)
                nc.gpsimd.tensor_tensor(x_sb[:, NT + t, :], x_sb[:, NT + t, :], xn[:, NT + t, :], ALU.add).then_inc(x1b_done, 1)
            split_wqk(1)
            for r in range(G // 2):
                store_v(r)
            pool.wait_ge(v_done, G)
            pool.wait_ge(wqk_split, 4)
            nc.gpsimd.memset(k1[1][DH:P, :].bitcast(F32), 1.0)
            nc.gpsimd.memset(qm[1][DH:P, :].bitcast(F32), 0.0).then_inc(stacks_cleared[1], 1)
            pool.wait_ge(stacks_cleared[1], 1)
            split_v(0, 0)

            def head(h, first=False, last=False, ahead=True):
                for b in range(B):
                    u = unit(h, b)
                    if b == B - 1 and ahead:
                        split_wqk(h + 2)
                    if not (last and b == B - 1):
                        split_v(u + 1, (b + 1) % B)
                    low_part(u)
                    if not (first and b == 0):
                        finish(u - 1, h if b else h - 1, (b + 1) % B)

            head(0, first=True)
            with pool.Fori(1, H - 2) as h:
                head(h)
            head(H - 2, ahead=False)
            head(H - 1, last=True, ahead=False)

        @block.scalar
        def _(act):
            act.wait_ge(ctx_turned, 1)
            act.copy(ctxT[:, :, :], psO[:, 0:C]).then_inc(ctx_kept, 1)
            act.copy(wkT[:, :, :], psO[:, HALF:HALF + CC * C]).then_inc(ctx_kept, 1)
            act.copy(wvT[:, :, :], psM[:, 0:CC * C]).then_inc(ctx_kept, 1)

            def keep_max(v):
                act.wait_ge(max_turned, v + 1)
                if not (isinstance(v, int) and v == 0):
                    act.wait_ge(max_set, 16 * v)
                act.copy(neg_max[:, :], psS[0:2 * NT, 0, 0:P]).then_inc(max_kept, 1)

            def std(n):
                act.wait_ge(eps_added, n + 1)
                part = rstd[:, (n % B) * NT:(n % B + 1) * NT]
                act.activation(part, part, ACT.Sqrt).then_inc(std_done, 1)

            std(0)
            std(1)
            act.wait_ge(kv1_done, 1)
            act.copy(kT1[:, :, :], psO[:, 0:C]).then_inc(kv1_kept, 1)
            act.copy(bq_col[:, :], psM[:, HALF:HALF + CC]).then_inc(kv1_kept, 1)
            act.wait_ge(v1_cleared, 1)
            for b in range(B):
                for odd in range(2):
                    act.copy(v1[odd * KEYS:(odd + 1) * KEYS, b, odd, :],
                             psO[b * KEYS:(b + 1) * KEYS, HALF:HALF + C]).then_inc(v1_spread, 1)

            def norm_half(n):
                act.wait_ge(shift_done, n - B + 1)
                for g in range(n % B * NT, NT if n == B else ACT_NORMS):
                    act.activation(xn[:, g, :], x_sb[:, g, :], ACT.Identity, bias=shift[:, g:g + 1],
                                   scale=rstd[:, g:g + 1]).then_inc(xn2_done, 1)

            def keep_xnT(k):
                act.wait_ge(xn_turned, k + 1)
                act.copy(xnT[:, :, 2 * k * P:(2 * k + 2) * P].rearrange("p c (g q) -> p g c q", q=P),
                         bank(k % 4).rearrange("p (g c q) -> p g c q", g=2, c=CC)).then_inc(xnT_kept, 1)

            def keep_xT_hi(k):
                act.wait_ge(xn_turned, G // 2 + k + 1)
                act.copy(xT_hi[:, :, 2 * k * P:(2 * k + 2) * P].rearrange("p c (g q) -> p g c q", q=P),
                         turned_bank(k).rearrange("p (g c q) -> p g c q", g=2, c=CC)).then_inc(xT_hi_kept, 1)

            for k in range(2):
                keep_xnT(k)
            act.wait_ge(fold_done, 1)
            act.copy(foldT[:, :, :], psM[:, 0:C]).then_inc(fold_kept, 1)
            act.copy(fold_b[:, :], psM[0:1, HALF:HALF + P]).then_inc(fold_kept, 1)
            for k in range(2, G // 2):
                keep_xnT(k)
            for b in range(B):
                act.wait_ge(sub1_done, b + 1)
                act.activation(prob1[:, b, :], prob1[:, b, :], ACT.Exp).then_inc(exp1_done, 1)
                act.wait_ge(prob1_turned, b + 1)
                act.copy(probT[:, b, :], bank(b)).then_inc(probT_kept, 1)

            def keep_qk_hi(z, b, src=psM):
                act.wait_ge(qk_done, z + 1)
                act.copy(qk_hi[b][:, :], src[:, :]).then_inc(qk_hi_kept, 1)

            act.wait_ge(rsum1_done, 2)
            for g in range(NT, G):
                act.wait_ge(out1_done, g // 2 + 1)
                act.activation(xn[:, g, :], pair_bank(g), ACT.Copy, scale=rsum1[:, g:g + 1]).then_inc(cross_kept, 1)
            std(2)
            norm_half(2)
            std(3)
            for k in range(G // 4):
                keep_xT_hi(k)
            norm_half(3)
            for k in range(G // 4, G // 2):
                keep_xT_hi(k)
            keep_qk_hi(0, 0, psM)
            keep_qk_hi(1, 1, psO)
            for c in range(4):
                act.wait_ge(logits_done, c + 1)
                act.copy(logits[:, c * HALF:(c + 1) * HALF], psM[0:2 * H, (c % 2) * HALF:(c % 2 + 1) * HALF]).then_inc(logits_kept, 1)
            act.wait_ge(logits_summed, 1)
            act.activation(g_exp[:, :, :], g_rank[:, :, :], ACT.Exp, scale=-1.0).then_inc(gate_exp, 1)
            for g in range(G):
                act.wait_ge(v_done, g + 1)
                r = g // 2
                if g % 2 == 0 and r >= STAGES:
                    act.wait_ge(v_stored[r % STAGES], 16 * (r // STAGES))
                act.copy(v_stage[:, r % STAGES, :, g % 2, :], bank(g % 4).rearrange("p (h d) -> p h d", d=DH)).then_inc(v_kept, 1)
                if g == FIRST_MAX + NT:
                    keep_max(0)
                if g == GATES_AT:
                    act.wait_ge(gate_turned, 1)
                    act.copy(g_unitT[:, :, :], psO[:, HALF:HALF + 3 * P]).then_inc(gate_row, 1)

            def keep_num(w):
                act.wait_ge(pv_done, NT * (w + 1))
                if not (isinstance(w, int) and w == 0):
                    act.wait_ge(out_split, 3 * w)
                    act.wait_ge(den_moved, 16 * w)
                    act.wait_ge(o_set, 32 * w)
                act.copy(num[:, :], psO[0:DH + 1, :]).then_inc(num_kept, 1)

            def head(h, first=False, last=False):
                for b in range(B):
                    u = unit(h, b)
                    if not (first and b == 0):
                        keep_max(u)
                    if not last:
                        keep_qk_hi(u + 2, b)
                    for t in range(NT):
                        act.wait_ge(scores_done, NT * u + t + 1)
                        if not (first and b == 0 and t < 2):
                            wait_lo(act, u, t - 2)
                        act.activation(prob[:, t % 2, :], psS[:, t % 2, :], ACT.Exp, scale=SCALE).then_inc(exp_done, 1)
                        act.wait_ge(exp_done, NT * u + t + 1)
                        if not (first and b == 0 and t < NPH):
                            act.wait_ge(pv_done, NT * u + t - NPH + 1)
                        act.copy(prob_hi[:, t % NPH, :], prob[:, t % 2, :]).then_inc(hi_done, 1)
                        if t == 0 and not (first and b == 0):
                            keep_num(u - 1)

            head(0, first=True)
            with act.Fori(1, H - 2) as h:
                head(h)
            head(H - 2)
            head(H - 1, last=True)
            act.wait_ge(pv_done, NT * U)
            act.copy(num_last, psO[0:DH + 1, :]).then_inc(num_kept, 1)

        @block.vector
        def _(dve):
            def norm_stats(n):
                for g in range(n % B * NT, (n % B + 1) * NT):
                    if n < B and g % 4 == 0:
                        dve.wait_ge(x_in[g // 4], 16)
                    if n >= B:
                        dve.wait_ge((x1_done, x1b_done)[n % B], g % NT + 1)
                    dve.bn_stats(stats[:, g, :], x_sb[:, g, :]).then_inc(stats_done, 1)
                for g in range(n % B * NT, (n % B + 1) * NT):
                    dve.wait_ge(stats_done, NT * n + g % NT + 1)
                    dve.bn_aggr(mean_var[:, g, :], stats[:, g, :]).then_inc(var_done, 1)
                half = slice(n % B * NT, (n % B + 1) * NT)
                dve.wait_ge(var_done, NT * (n + 1))
                dve.tensor_scalar(rstd[:, half], mean_var[:, half, 1], LN_EPS, None, ALU.add).then_inc(eps_added, 1)

            def norm_half(n):
                half = slice(n % B * NT, (n % B + 1) * NT)
                dve.wait_ge(std_done, n + 1)
                dve.reciprocal(rstd[:, half], rstd[:, half]).then_inc(rstd_done, 1)
                dve.wait_ge(rstd_done, n + 1)
                if n >= B:
                    dve.scalar_tensor_tensor(out=shift[:, half], in0=mean_var[:, half, 0], scalar=-1.0, in1=rstd[:, half],
                                             op0=ALU.mult, op1=ALU.mult).then_inc(shift_done, 1)
                if n == B:
                    return
                for g in range(n * NT if n < B else ACT_NORMS, (n % B + 1) * NT):
                    dve.tensor_scalar(xn[:, g, :], x_sb[:, g, :], mean_var[:, g, 0:1], rstd[:, g:g + 1],
                                      ALU.subtract, ALU.mult).then_inc(xn_done, 1)

            dve.memset(v1[:, :, :, :], 0.0).then_inc(v1_cleared, 1)
            norm_stats(0)
            norm_stats(1)
            norm_half(0)
            norm_half(1)
            dve.memset(k1[0][DH:P, :].bitcast(F32), 1.0)
            dve.memset(qm[0][DH:P, :].bitcast(F32), 0.0).then_inc(stacks_cleared[0], 1)
            def weights1(b):
                half = slice(b * NT, (b + 1) * NT)
                dve.wait_ge(exp1_done, b + 1)
                dve.reduce_sum(sum1[:, half], prob1[:, b, :].rearrange("p (t k) -> p t k", k=KEYS), AX.X).then_inc(sum1_done, 1)
                dve.wait_ge(sum1_done, b + 1)
                dve.reciprocal(rsum1[:, half], sum1[:, half]).then_inc(rsum1_done, 1)

            def add_cross():
                dve.wait_ge(rsum1_done, 1)
                for g in range(NT):
                    dve.wait_ge(out1_done, g // 2 + 1)
                    dve.scalar_tensor_tensor(out=x_sb[:, g, :], in0=pair_bank(g), scalar=rsum1[:, g:g + 1],
                                             in1=x_sb[:, g, :], op0=ALU.mult, op1=ALU.add).then_inc(x1_done, 1)

            def keep_xT_lo(k):
                dve.wait_ge(xT_hi_kept, k + 1)
                view = slice(2 * k * P, (2 * k + 2) * P)
                dve.tensor_tensor(xT_lo[:, :, view].rearrange("p c (g q) -> p g c q", q=P),
                                  turned_bank(k).rearrange("p (g c q) -> p g c q", g=2, c=CC),
                                  xT_hi[:, :, view].rearrange("p c (g q) -> p g c q", q=P),
                                  ALU.subtract).then_inc(xT_lo_kept, 1)

            for b in range(B):
                half = slice(b * NT, (b + 1) * NT)
                dve.wait_ge(sc1_done, b + 1)
                scores1 = psM[:, b * HALF:(b + 1) * HALF].rearrange("p (t k) -> p t k", k=KEYS)
                dve.reduce_max(mx1[:, half], scores1, AX.X).then_inc(max1_done, 1)
                dve.wait_ge(max1_done, b + 1)
                dve.tensor_tensor(prob1[:, b, :].rearrange("p (t k) -> p t k", k=KEYS), scores1,
                                  mx1[:, half].unsqueeze(2).broadcast_to([P, NT, KEYS]), ALU.subtract).then_inc(sub1_done, 1)
                if b == 0:
                    weights1(0)
            add_cross()
            weights1(1)
            norm_stats(2)
            norm_half(2)
            norm_stats(3)
            norm_half(3)
            for k in range(G // 2):
                keep_xT_lo(k)

            def keep_qk_lo(z, b, src=psM):
                dve.wait_ge(qk_hi_kept, z + 1)
                dve.tensor_tensor(qk_lo[b][:, :], src[:, :], qk_hi[b][:, :], ALU.subtract).then_inc(qk_lo_kept, 1)

            keep_qk_lo(0, 0, psM)
            keep_qk_lo(1, 1, psO)

            def find_max(v, b, t):
                dve.wait_ge(max_scores, NT * v + t + 1)
                dve.reduce_max(row_max[:, b, t:t + 1], psM[:, :], AX.X).then_inc(max_found, 1)

            def split_max(v, b):
                dve.wait_ge(max_found, NT * (v + 1))
                if not (isinstance(v, int) and v == 0):
                    dve.wait_ge(max_turned, v)
                dve.tensor_scalar(max_parts[:, 0, :], row_max[:, b, :], -1.0, None, ALU.mult).then_inc(max_split, 1)
                dve.wait_ge(max_split, 2 * v + 1)
                dve.scalar_tensor_tensor(out=max_parts[:, 1, :], in0=row_max[:, b, :], scalar=-1.0, in1=max_parts[:, 0, :],
                                         op0=ALU.mult, op1=ALU.subtract).then_inc(max_split, 1)

            dve.wait_ge(logits_turned, 1)
            dve.reduce_sum(g_rank[:, :, :], psO[:, 0:2 * G * H].rearrange("p (g a h) -> p g h a", a=2, h=H), AX.X).then_inc(logits_summed, 1)
            dve.wait_ge(gate_exp, 1)
            dve.tensor_scalar(g_exp[:, :, :], g_exp[:, :, :], 1.0, None, ALU.add).then_inc(gate_step, 1)
            dve.wait_ge(gate_step, 1)
            dve.reciprocal(g_sig[:, :, :], g_exp[:, :, :]).then_inc(gate_step, 1)
            dve.wait_ge(gate_step, 2)
            ahead = xn[:, 0:4, :].rearrange("p g c -> p (g c)").rearrange("p (g h k) -> p g h k", h=H, k=H)
            tied = xn[:, 4:8, :].rearrange("p g c -> p (g c)").rearrange("p (g h k) -> p g h k", h=H, k=H)
            other = g_sig[:, :, :].unsqueeze(2).broadcast_to([P, G, H, H])
            own = g_sig[:, :, :].unsqueeze(3).broadcast_to([P, G, H, H])
            dve.wait_ge(xn_turned, G)
            dve.tensor_tensor(ahead, other, own, ALU.is_gt).then_inc(gate_step, 1)
            dve.tensor_tensor(tied, other, own, ALU.is_equal).then_inc(gate_step, 1)
            dve.wait_ge(gate_step, 4)
            dve.wait_ge(consts_done, 4)
            dve.tensor_tensor(tied, tied, before[:, :, :].unsqueeze(1).broadcast_to([P, G, H, H]), ALU.mult).then_inc(gate_step, 1)
            dve.wait_ge(gate_step, 5)
            dve.tensor_tensor(ahead, ahead, tied, ALU.add).then_inc(gate_step, 1)
            dve.wait_ge(gate_step, 6)
            dve.reduce_sum(g_rank[:, :, :], ahead, AX.X).then_inc(gate_step, 1)
            dve.wait_ge(gate_step, 7)
            dve.tensor_scalar(g_rank[:, :, :], g_rank[:, :, :], float(TOP_K), None, ALU.is_lt).then_inc(gate_step, 1)
            dve.wait_ge(gate_step, 8)
            dve.tensor_tensor(g_unit[:, :].rearrange("p (h b t) -> p b t h", b=B, t=NT),
                              g_rank[:, :, :].rearrange("p (b t) h -> p b t h", b=B),
                              g_sig[:, :, :].rearrange("p (b t) h -> p b t h", b=B), ALU.mult).then_inc(gate_step, 1)
            dve.wait_ge(gate_step, 9)
            dve.tensor_copy(g_hi[:, :], g_unit[:, :]).then_inc(gate_step, 1)
            dve.wait_ge(gate_step, 10)
            dve.tensor_tensor(g_lo[:, :], g_unit[:, :], g_hi[:, :], ALU.subtract).then_inc(gate_step, 1)
            def add_bias(r):
                dve.wait_ge(bias_done, r + 1)
                two = x_sb[:, 2 * r:2 * r + 2, :]
                dve.tensor_tensor(two, psO[:, (r % 2) * HALF:(r % 2 + 1) * HALF].rearrange("p (g c) -> p g c", c=C),
                                  two, ALU.add).then_inc(base_done, 1)

            for g in range(FIRST_MAX, G):
                if g < FIRST_MAX + NT:
                    find_max(0, 0, g - FIRST_MAX)
                if g == FIRST_MAX + NT:
                    split_max(0, 0)
                if g >= BIAS_AT:
                    add_bias(g - BIAS_AT)
            for r in range(G - BIAS_AT, G // 2):
                add_bias(r)

            def low_part(u, t):
                dve.wait_ge(hi_done, NT * u + t + 1)
                if not (isinstance(u, int) and NT * u + t < 2):
                    dve.wait_ge(pv_done, NT * u + t - 1)
                t = t % NT
                dve.tensor_tensor(prob_lo[:, t % 2, :], prob[:, t % 2, :], prob_hi[:, t % NPH, :], ALU.subtract).then_inc(lo_done, 1)

            def split_wo(n):
                some = slice(n * H // 4, (n + 1) * H // 4)
                dve.tensor_tensor(wo_lo[:, some, :], wo_raw[:, some, :], wo_hi[:, some, :], ALU.subtract).then_inc(wo_split, 1)

            def weigh(w):
                dve.wait_ge(den_moved, 16 * (w + 1))
                dve.reciprocal(rden[:, :], den[:, :]).then_inc(rden_done, 1)
                dve.wait_ge(rden_done, w + 1)
                dve.wait_ge(gate_fetched, 16 * (w + 1))
                if not (isinstance(w, int) and w == 0):
                    dve.wait_ge(weight_stored, 16 * w)
                dve.tensor_tensor(weight[:, :], rden[:, :], gate[:, :], ALU.mult).then_inc(weight_done, 1)

            def head(h, first=False, last=False):
                for b in range(B):
                    u = unit(h, b)
                    more = not (last and b == B - 1)
                    if not (first and b == 0):
                        split_max(u, b)
                        low_part(u, -1)
                    if not more:
                        split_wo(2)
                        split_wo(3)
                    if not last:
                        keep_qk_lo(u + 2, b)
                    for t in range(NT):
                        if more:
                            find_max(u + 1, (b + 1) % B, t)
                        if t != POOL_TILE and t < NT - 1:
                            low_part(u, t)
                        if t == (WEIGH_AT if more else WEIGH_AT - 1) and not (first and b == 0):
                            weigh(u - 1)
                        if last and b == 0 and t == 4:
                            dve.wait_ge(wo_landed, 32)
                            dve.tensor_copy(wo_hi[:, :, :], wo_raw[:, :, :]).then_inc(wo_split, 1)
                            dve.wait_ge(wo_split, 1)
                        if last and b == 0 and 4 < t < 7:
                            split_wo(t - 5)
            head(0, first=True)
            with dve.Fori(1, H - 2) as h:
                head(h)
            head(H - 2)
            head(H - 1, last=True)
            low_part(U, -1)
            weigh(U - 1)

            def finish_tile(g):
                dve.wait_ge(proj_done, g + 1)
                base = (base0, base1)[g // NT]
                src = final_half(g)
                dve.tensor_tensor(base[:, g % NT, :], src, base[:, g % NT, :], ALU.add).then_inc(final_done, 1)

            dve.wait_ge(base_fetched, 32)
            for g in range(NT // 2):
                finish_tile(g)
            dve.wait_ge(wide_fetched, 16 * U)
            dve.tensor_tensor(o_hi_last, num_last[0:DH, :], wide_last, ALU.mult).then_inc(last_split, 1)
            dve.tensor_tensor(num_last[0:DH, :], num_last[0:DH, :], wide_last, ALU.mult).then_inc(last_split, 1)
            dve.wait_ge(last_split, 2)
            dve.tensor_tensor(num_last[0:DH, :], num_last[0:DH, :], o_hi_last, ALU.subtract).then_inc(last_split, 1)
            for g in range(NT // 2, G):
                finish_tile(g)

        @block.tensor
        def _(pe):
            pe.wait_ge(consts_done, 4)
            pe.wait_ge(ctx_landed, 16 * 7)
            for cc in range(CC):
                pe.transpose(psO[:, cc * P:(cc + 1) * P], ctx_sb[:, cc * P:(cc + 1) * P], ident[:, :])
            for ps, w_sb in ((psO[:, HALF:2 * HALF], wk_sb), (psM[:, 0:HALF], wv_sb)):
                for cc in range(CC):
                    for dd in range(CC):
                        mm = pe.transpose(ps[:, cc * C + dd * P:cc * C + (dd + 1) * P],
                                          w_sb[:, dd, cc * P:(cc + 1) * P], ident[:, :])
            mm.then_inc(ctx_turned, 1)
            def turn_xn(n, k):
                if n == 0:
                    pe.wait_ge(xn_done, 2 * k + 2)
                elif 2 * k < ACT_NORMS:
                    pe.wait_ge(xn2_done, 2 * k + 2)
                else:
                    pe.wait_ge(xn_done, G + 2 * k + 2 - ACT_NORMS)
                if n == 0 and k >= 4:
                    pe.wait_ge(xnT_kept, k - 3)
                if n == 1 and k == 3:
                    pe.wait_ge(cross_kept, 4)
                if n == 1 and k == 4:
                    pe.wait_ge(cross_kept, 8)
                if n == 1 and k >= 6:
                    pe.wait_ge(xT_lo_kept, k - 5)
                dst = turned_bank(k) if n else bank(k % 4)
                for j in range(2):
                    for cc in range(CC):
                        mm = pe.transpose(dst[:, (j * CC + cc) * P:(j * CC + cc + 1) * P],
                                          xn[:, 2 * k + j, cc * P:(cc + 1) * P], ident[:, :])
                mm.then_inc(xn_turned, 1)

            pe.wait_ge(ctx_kept, 3)
            for dd in range(CC):
                for cc in range(CC):
                    pe.matmul(psO[:, dd * P:(dd + 1) * P], wkT[:, cc, dd * P:(dd + 1) * P], ctxT[:, cc, :],
                              start=(cc == 0), stop=False)
                pe.matmul(psO[:, dd * P:(dd + 1) * P], bk_sb[:, dd * P:(dd + 1) * P], ones_row[:, :],
                          start=False, stop=True)
                pe.matmul(psM[:, HALF + dd:HALF + dd + 1], bq_sb[:, dd * P:(dd + 1) * P], ones_row[:, 0:1],
                          start=True, stop=True)
            for cc in range(CC):
                pe.matmul(psO[:, HALF:HALF + C], ctxT[:, cc, :], wvT[:, cc, :], start=(cc == 0), stop=False)
            pe.matmul(psO[:, HALF:HALF + C], ones_row[:, :], bv_sb[:, :], start=False, stop=True).then_inc(kv1_done, 1)
            for k in range(2):
                turn_xn(0, k)
            pe.wait_ge(kv1_kept, 2)
            for cc in range(CC):
                for dd in range(CC):
                    pe.matmul(psM[:, cc * P:(cc + 1) * P], wq_sb[:, dd, cc * P:(cc + 1) * P], kT1[:, dd, :],
                              start=(dd == 0), stop=(dd == CC - 1))
            for dd in range(CC):
                mm = pe.matmul(psM[0:1, HALF:HALF + P], bq_col[:, dd:dd + 1], kT1[:, dd, :],
                               start=(dd == 0), stop=(dd == CC - 1))
            mm.then_inc(fold_done, 1)

            for k in range(2, G // 2):
                turn_xn(0, k)
            def turn_prob(b):
                pe.wait_ge(exp1_done, b + 1)
                for pair in range(NT // 2):
                    mm = pe.transpose(bank(b)[:, pair * P:(pair + 1) * P], prob1[:, b, pair * P:(pair + 1) * P], ident[:, :])
                mm.then_inc(prob1_turned, 1)

            pe.wait_ge(fold_kept, 2)
            for b in range(B):
                pe.wait_ge(xnT_kept, G // 4 * (b + 1))
                keys = slice(b * KEYS, (b + 1) * KEYS)
                pe.matmul(psM[:, b * HALF:(b + 1) * HALF], ones_row[:, :],
                          fold_b[:, keys].unsqueeze(1).broadcast_to([1, NT, KEYS]), start=True, stop=False)
                for t in range(NT):
                    if b == 1 and t == NT // 2:
                        turn_prob(0)
                    g = b * NT + t
                    for cc in range(CC):
                        mm = pe.matmul(psM[:, b * HALF + t * KEYS:b * HALF + (t + 1) * KEYS],
                                       xnT[:, cc, g * P:(g + 1) * P], foldT[:, cc, keys],
                                       start=False, stop=(t == NT - 1 and cc == CC - 1))
                mm.then_inc(sc1_done, 1)
            pe.wait_ge(v1_spread, 2 * B)

            def out1(b):
                for g in range(b * NT, (b + 1) * NT, 2):
                    if g >= 8:
                        pe.wait_ge(x1_done, g - 6)
                    t = g % NT
                    for odd in range(2):
                        mm = pe.matmul(pair_bank(g + odd), probT[:, b, t // 2 * P:(t // 2 + 1) * P], v1[:, b, odd, :],
                                       start=True, stop=True)
                    mm.then_inc(out1_done, 1)

            pe.wait_ge(probT_kept, 1)
            out1(0)
            turn_prob(1)
            pe.wait_ge(probT_kept, 2)
            out1(1)
            for k in range(G // 2):
                turn_xn(1, k)

            def project(z, b, dst=psM):
                for n, (w, xT) in enumerate(((wqk_hi, xT_hi), (wqk_hi, xT_lo), (wqk_lo, xT_hi))):
                    for cc in range(CC):
                        for half in range(NH):
                            mm = pe.matmul(dst[:, half * HALF:(half + 1) * HALF], w[:, cc, :],
                                           xT[:, cc, b * T + half * HALF:b * T + (half + 1) * HALF],
                                           start=(n == 0 and cc == 0), stop=(n == 2 and cc == CC - 1))
                mm.then_inc(qk_done, 1)

            def max_tile(v, b, t):
                for half in range(NH):
                    mm = pe.matmul(psM[:, half * HALF:(half + 1) * HALF], qq[b][:, t * P:(t + 1) * P],
                                   kk[b][:, half * HALF:(half + 1) * HALF], start=True, stop=True)
                mm.then_inc(max_scores, 1)

            def turn_max(v):
                pe.wait_ge(max_split, 2 * (v + 1))
                if not (isinstance(v, int) and v == 0):
                    pe.wait_ge(exp_done, NT * v - 1)
                pe.transpose(psS[0:2 * NT, 0, 0:P], max_parts[:, :, :].rearrange("p a t -> p (a t)").bitcast(F32),
                             ident[:, :]).then_inc(max_turned, 1)

            pe.wait_ge(xT_lo_kept, G // 4)
            pe.wait_ge(wqk_split, 2)
            project(0, 0, psM)
            pe.wait_ge(xT_lo_kept, G // 2)
            project(1, 1, psO)
            pe.wait_ge(ws_split, 2)
            pe.wait_ge(qk_lo_kept, 1)
            for c in range(4):
                if c >= 2:
                    pe.wait_ge(logits_kept, c - 1)
                for xT in (xT_hi, xT_lo):
                    for cc in range(CC):
                        mm = pe.matmul(psM[0:2 * H, (c % 2) * HALF:(c % 2 + 1) * HALF], ws_parts[:, cc, :, :].rearrange("p a h -> p (a h)"),
                                       xT[:, cc, c * HALF:(c + 1) * HALF],
                                       start=(xT is xT_hi and cc == 0), stop=(xT is xT_lo and cc == CC - 1))
                mm.then_inc(logits_done, 1)

            def gate_bias(r):
                if r == 0:
                    pe.wait_ge(gates_back, 64)
                    pe.wait_ge(bo_split, 2)
                if r >= 2:
                    pe.wait_ge(base_done, r - 1)
                for g in (2 * r, 2 * r + 1):
                    dst = psO[:, (r % 2) * HALF + g % 2 * C:(r % 2) * HALF + (g % 2 + 1) * C]
                    mm = pe.matmul(dst, gate_st[:, g * P:(g + 1) * P], bo_st[:, :], start=True, stop=True)
                mm.then_inc(bias_done, 1)

            pe.wait_ge(wv_split, 2)
            for g in range(G):
                if g >= 4:
                    pe.wait_ge(v_kept, g - 3)
                terms = ((xT_hi, wv_hi), (xT_hi, wv_lo), (xT_lo, wv_hi))
                for n, (xT, w) in enumerate(terms):
                    for cc in range(CC):
                        mm = pe.matmul(bank(g % 4), xT[:, cc, g * P:(g + 1) * P], w[:, cc, :],
                                       start=(n == 0 and cc == 0), stop=(n == 2 and cc == CC - 1))
                mm.then_inc(v_done, 1)
                if g == 0:
                    pe.wait_ge(logits_kept, 4)
                    pe.wait_ge(qk_lo_kept, 2)
                    for j in range(G):
                        mm = pe.transpose(psO[:, 2 * j * H:2 * (j + 1) * H], logits[:, j * P:(j + 1) * P],
                                          ident[0:2 * H, 0:2 * H])
                    mm.then_inc(logits_turned, 1)
                t = g - FIRST_MAX
                if t == 0:
                    pe.wait_ge(pairs_set, 64)
                if 0 <= t < NT:
                    if t:
                        pe.wait_ge(max_found, t)
                    max_tile(0, 0, t)
                if t == NT:
                    pe.wait_ge(v_kept, 13)
                    turn_max(0)
                if g == GATES_AT:
                    pe.wait_ge(gate_step, 11)
                    for part, src in enumerate((g_unit[:, :], g_hi[:, :].bitcast(F32), g_lo[:, :].bitcast(F32))):
                        mm = pe.transpose(psO[:, HALF + part * P:HALF + (part + 1) * P], src, ident[:, :])
                    mm.then_inc(gate_turned, 1)
                if g >= BIAS_AT:
                    gate_bias(g - BIAS_AT)
            for r in range(G - BIAS_AT, G // 2):
                gate_bias(r)
            pe.wait_ge(v_kept, G)

            def score_pairs(u, b, t, first):
                if not (first and t < 2):
                    pe.wait_ge(exp_done, NT * u + t - 1)
                for half in range(NH):
                    pe.matmul(psS[:, t % 2, half * HALF:(half + 1) * HALF], kk[b][:, t * P:(t + 1) * P],
                              qq[b][:, half * HALF:(half + 1) * HALF], start=True, stop=False)

            def score_rest(u, b, t):
                if t == 0:
                    pe.wait_ge(max_set, 16 * (u + 1))
                for half in range(NH):
                    mm = pe.matmul(psS[:, t % 2, half * HALF:(half + 1) * HALF], k1[b][:, t * P:(t + 1) * P],
                                   qm[b][:, half * HALF:(half + 1) * HALF], start=False, stop=True)
                mm.then_inc(scores_done, 1)

            def pv_tile(w, b, t, between=None):
                if t == 0:
                    pe.wait_ge(v_split, 2 * (w + 1))
                    if isinstance(w, int) and w == 0:
                        pe.wait_ge(base_done, NT)
                    else:
                        pe.wait_ge(num_kept, w)
                wait_lo(pe, w, t)
                hi, lo = prob_hi[:, t % NPH, :], prob_lo[:, t % 2, :]
                with_ones, v_lo = v_st[b][:, t, 0:DH + 2], v_st[b][:, t, VLO:VLO + DH]
                for half in range(NH):
                    mm = pe.matmul(psO[0:DH + 2, half * HALF:(half + 1) * HALF], with_ones,
                                   hi[:, half * HALF:(half + 1) * HALF], start=(t == 0), stop=False)
                    if t == NT - 1 - LAG and half == 0:
                        mm.then_inc(stacks_free, 1)
                for half in range(NH):
                    pe.matmul(psO[0:DH, half * HALF:(half + 1) * HALF], v_lo,
                              hi[:, half * HALF:(half + 1) * HALF], start=False, stop=False)
                if between:
                    between()
                for half in range(NH):
                    mm = pe.matmul(psO[0:DH + 2, half * HALF:(half + 1) * HALF], with_ones,
                                   lo[:, half * HALF:(half + 1) * HALF], start=False, stop=(t == NT - 1))
                mm.then_inc(pv_done, 1)

            def project_out(g, heads):
                b, t = divmod(g, NT)
                for h in heads:
                    for w in (wo_hi, wo_lo):
                        mm = pe.matmul(final_half(g), o_st[:, b, h, t * P:(t + 1) * P], w[:, h, :],
                                       start=(h == 0 and w is wo_hi), stop=(h == H - 1 and w is wo_lo))
                return mm

            def head(h, first=False, last=False):
                for b in range(B):
                    u = unit(h, b)
                    more = not (last and b == B - 1)

                    def next_max(m):
                        if not more:
                            return
                        if m == 0:
                            pe.wait_ge(pairs_set, 64 * (u + 2))
                            if last:
                                pe.wait_ge(qk_lo_kept, U)
                            else:
                                pe.wait_ge(qk_lo_kept, u + 3)
                        else:
                            pe.wait_ge(max_found, NT * (u + 1) + m)
                        max_tile(u + 1, (b + 1) % B, m)

                    before_it = not (first and b == 0)
                    if before_it:
                        pv_tile(u - 1, (b + 1) % B, NT - LAG)
                        turn_max(u)
                    if not more:
                        pe.wait_ge(wo_split, 5)
                        pe.wait_ge(o_set, 32 * (U - B - 1))
                        project_out(0, range(H - 1))
                    pe.wait_ge(rest_set[b], 32 * (h + 1))
                    if not last:
                        if b == 0:
                            pe.wait_ge(wqk_split, 2 * (h + 2))
                        project(u + 2, b)
                    pe.wait_ge(max_kept, u + 1)
                    score_pairs(u, b, 0, first and b == 0)
                    score_rest(u, b, 0)
                    if before_it:
                        pv_tile(u - 1, (b + 1) % B, NT - 1)
                    next_max(0)
                    for t in range(1, NT):
                        score_pairs(u, b, t, first and b == 0)
                        score_rest(u, b, t)
                        if t == LAG:
                            next_max(1)
                        if t == LAG and not more:
                            project_out(1, range(H - 1))
                        if t >= LAG:
                            pv_tile(u, b, t - LAG, lambda: next_max(t))

            head(0, first=True)
            with pe.Fori(1, H - 2) as h:
                head(h)
            head(H - 2)
            head(H - 1, last=True)
            for t in range(NT - LAG, NT):
                pv_tile(U - 1, B - 1, t)
            for g in range(2, 6):
                project_out(g, range(H - 1))
            pe.wait_ge(o_set, 32 * (U - 1))
            for g in range(6):
                project_out(g, range(H - 1, H)).then_inc(proj_done, 1)
            for g in range(6, NT):
                pe.wait_ge(final_done, g - 3)
                project_out(g, range(H)).then_inc(proj_done, 1)
            pe.wait_ge(final_done, 2)
            pe.wait_ge(num_kept, U)
            for g in range(NT, NT + 4):
                project_out(g, range(H - 1))
            pe.wait_ge(last_o_set, 32)
            for g in range(NT, NT + 4):
                project_out(g, range(H - 1, H)).then_inc(proj_done, 1)
            pe.wait_ge(final_done, NT)
            for g in range(NT + 4, G):
                project_out(g, range(H)).then_inc(proj_done, 1)


_INS = ['x', 'ctx_1024', 'L0_xattn_Wq', 'L0_xattn_bq', 'L0_xattn_Wk', 'L0_xattn_bk', 'L0_xattn_Wv',
        'L0_xattn_bv', 'L0_ffn_Wq', 'L0_ffn_Wkv', 'L0_ffn_Ws', 'L0_ffn_Wo', 'L0_ffn_bo']


def kernel(**inputs):
    import numpy as _np
    import concourse.bacc as _bacc
    from concourse import mybir as _mybir
    from concourse.bass_utils import run_bass_kernel_spmd as _run

    nc = _bacc.Bacc("TRN2", target_bir_lowering=False, num_devices=1)
    arrays, args = {}, []
    for name in _INS:
        a = _np.ascontiguousarray(inputs[name])
        arrays[f"in_{name}_dram"] = a
        args.append(nc.dram_tensor(f"in_{name}_dram", a.shape, _mybir.dt.from_np(a.dtype), kind="ExternalInput").ap())
    shape = inputs['x'].shape
    args.append(nc.dram_tensor("out_0_dram", shape, _mybir.dt.from_np(_np.dtype("float32")), kind="ExternalOutput").ap())
    build(nc, *args)
    r = _run(nc, [arrays], core_ids=[0])
    return r.results[0]["out_0_dram"]
```
